# Optimizing a Trainium2 kernel written in Bass

```python
import numpy as np
import jax
import jax.numpy as jnp

def _softmax(x, axis=-1):
    return jax.nn.softmax(x, axis=axis)

def _gelu(x):
    return jax.nn.gelu(x, approximate=True)

def _silu(x):
    return jax.nn.silu(x)

def _sigmoid(x):
    return jax.nn.sigmoid(x)

def _layernorm(x, axis=-1, eps=1e-05):
    m = jnp.mean(x, axis=axis, keepdims=True)
    v = jnp.var(x, axis=axis, keepdims=True)
    return (x - m) / jnp.sqrt(v + eps)

def _scatter_add(tgt, idx, src, axis=0):
    return tgt.at[idx].add(src)

def _segment_sum(src, seg, n):
    return jax.ops.segment_sum(src, seg, n)
kernel_name = 'mk_conv_seq_d2_conv_nchw128_r2_b4e403'

def setup_inputs(seed: int=0):
    np.random.seed(seed)
    _w = jnp.asarray

    def _rec_inputs():
        import jax
        import jax.numpy as jnp
        _gk = jax.random.key(seed)
        x = -0.000125 + 0.9999 * jax.random.normal(jax.random.fold_in(_gk, 1), (16, 64, 64, 64), jnp.float32)
        return x
    x = _rec_inputs()

    def _L0_conv_setup():
        import jax, jax.numpy as jnp
        import numpy as np
        from jax import lax
        H_STEP = 1.0 / 3.0
        N_STEPS = 3

        def _conv(x, w):
            return lax.conv_general_dilated(x, w, window_strides=(1, 1), padding='SAME', dimension_numbers=('NCHW', 'OIHW', 'NCHW'))
        key = jax.random.key(seed)
        ks = jax.random.split(key, 5)
        B, C, H, W = (16, 64, 64, 64)
        fan_in = C * 9
        return {'x': jax.random.normal(ks[0], (B, C, H, W), dtype=jnp.float32), 'w1': jax.random.normal(ks[1], (C, C, 3, 3), dtype=jnp.float32) * (2.0 / fan_in) ** 0.5, 'b1': jax.random.normal(ks[2], (C,), dtype=jnp.float32) * 0.01, 'w2': jax.random.normal(ks[3], (C, C, 3, 3), dtype=jnp.float32) * (2.0 / fan_in) ** 0.5, 'b2': jax.random.normal(ks[4], (C,), dtype=jnp.float32) * 0.01}
    _L0_conv_all = _L0_conv_setup()
    _L0_conv_in = {k: v for k, v in _L0_conv_all.items() if k in ('w1', 'b1', 'w2', 'b2')}
    del _L0_conv_all

    def _L1_conv_setup():
        import jax, jax.numpy as jnp
        import numpy as np
        MIDC = 64
        HEADS = 8
        HEADC = MIDC // HEADS
        EPS = 1e-05

        def _ln(t, w, b):
            m = t.mean(-1, keepdims=True)
            s = jnp.std(t, axis=-1, ddof=1, keepdims=True)
            return w * ((t - m) / (s + EPS)) + b
        key = jax.random.key(seed)
        ks = jax.random.split(key, 8)
        B, C, H, W = (8, MIDC, 128, 128)
        s = 1.0 / np.sqrt(C)
        x = jax.random.normal(ks[0], (B, C, H, W), dtype=jnp.float32)
        qkv_w = jax.random.normal(ks[1], (3 * C, C), dtype=jnp.float32) * s
        o1_w = jax.random.normal(ks[2], (C, C), dtype=jnp.float32) * s
        o2_w = jax.random.normal(ks[3], (C, C), dtype=jnp.float32) * s
        kln_w = 1.0 + 0.1 * jax.random.normal(ks[4], (HEADS, 1, HEADC), dtype=jnp.float32)
        kln_b = 0.1 * jax.random.normal(ks[5], (HEADS, 1, HEADC), dtype=jnp.float32)
        vln_w = 1.0 + 0.1 * jax.random.normal(ks[6], (HEADS, 1, HEADC), dtype=jnp.float32)
        vln_b = 0.1 * jax.random.normal(ks[7], (HEADS, 1, HEADC), dtype=jnp.float32)
        return {'x': x, 'qkv_w': qkv_w, 'o1_w': o1_w, 'o2_w': o2_w, 'kln_w': kln_w, 'kln_b': kln_b, 'vln_w': vln_w, 'vln_b': vln_b}
    _L1_conv_all = _L1_conv_setup()
    _L1_conv_in = {k: v for k, v in _L1_conv_all.items() if k in ('qkv_w', 'o1_w', 'o2_w', 'kln_w', 'kln_b', 'vln_w', 'vln_b')}
    del _L1_conv_all
    return {'x': x, 'L0_conv_w1': _L0_conv_in['w1'], 'L0_conv_b1': _L0_conv_in['b1'], 'L0_conv_w2': _L0_conv_in['w2'], 'L0_conv_b2': _L0_conv_in['b2'], 'L1_conv_qkv_w': _L1_conv_in['qkv_w'], 'L1_conv_o1_w': _L1_conv_in['o1_w'], 'L1_conv_o2_w': _L1_conv_in['o2_w'], 'L1_conv_kln_w': _L1_conv_in['kln_w'], 'L1_conv_kln_b': _L1_conv_in['kln_b'], 'L1_conv_vln_w': _L1_conv_in['vln_w'], 'L1_conv_vln_b': _L1_conv_in['vln_b']}

def reference(x, L0_conv_w1, L0_conv_b1, L0_conv_w2, L0_conv_b2, L1_conv_qkv_w, L1_conv_o1_w, L1_conv_o2_w, L1_conv_kln_w, L1_conv_kln_b, L1_conv_vln_w, L1_conv_vln_b):
    import jax
    import jax.numpy as jnp

    def _L0_conv_ref(x, w1, b1, w2, b2):
        import jax, jax.numpy as jnp
        import numpy as np
        from jax import lax
        H_STEP = 1.0 / 3.0
        N_STEPS = 3

        def _conv(x, w):
            return lax.conv_general_dilated(x, w, window_strides=(1, 1), padding='SAME', dimension_numbers=('NCHW', 'OIHW', 'NCHW'))
        for _ in range(N_STEPS):
            t = jax.nn.relu(_conv(x, w1) + b1[None, :, None, None])
            x = x + H_STEP * (_conv(t, w2) + b2[None, :, None, None])
        return jax.nn.relu(x)

    def _L1_conv_ref(x, qkv_w, o1_w, o2_w, kln_w, kln_b, vln_w, vln_b):
        import jax, jax.numpy as jnp
        import numpy as np
        MIDC = 64
        HEADS = 8
        HEADC = MIDC // HEADS
        EPS = 1e-05

        def _ln(t, w, b):
            m = t.mean(-1, keepdims=True)
            s = jnp.std(t, axis=-1, ddof=1, keepdims=True)
            return w * ((t - m) / (s + EPS)) + b
        B, C, H, W = x.shape
        hc = C // HEADS
        N = H * W
        qkv = jnp.einsum('oc,bchw->bhwo', qkv_w, x)
        qkv = qkv.reshape(B, N, HEADS, 3 * hc).transpose(0, 2, 1, 3)
        q, k, v = jnp.split(qkv, 3, axis=-1)
        k = _ln(k, kln_w, kln_b)
        v = _ln(v, vln_w, vln_b)
        kv = jnp.einsum('bhnd,bhne->bhde', k, v) / N
        o = jnp.einsum('bhnd,bhde->bhne', q, kv)
        o = o.transpose(0, 2, 1, 3).reshape(B, H, W, C).transpose(0, 3, 1, 2)
        ret = o + x
        u = jnp.einsum('oc,bchw->bohw', o1_w, ret)
        u = jax.nn.gelu(u, approximate=False)
        u = jnp.einsum('oc,bchw->bohw', o2_w, u) + x
        return jax.nn.gelu(u, approximate=False)

    def _gn(v, G=32, eps=1e-05):
        B_, C_, H_, W_ = v.shape
        g = v.reshape(B_, G, C_ // G, H_, W_)
        m = jnp.mean(g, axis=(2, 3, 4), keepdims=True)
        s = jnp.var(g, axis=(2, 3, 4), keepdims=True)
        return ((g - m) / jnp.sqrt(s + eps)).reshape(v.shape)

    def _ln_c(v, eps=1e-06):
        m = jnp.mean(v, axis=1, keepdims=True)
        s = jnp.var(v, axis=1, keepdims=True)
        return (v - m) / jnp.sqrt(s + eps)

    def _ln_t(v, eps=1e-05):
        m = jnp.mean(v, axis=-1, keepdims=True)
        s = jnp.var(v, axis=-1, keepdims=True)
        return (v - m) / jnp.sqrt(s + eps)

    def _to_tokens(v):
        B_, C_, H_, W_ = v.shape
        return v.reshape(B_, C_, H_ * W_).transpose(0, 2, 1)

    def _from_tokens(t, like):
        B_, C_, H_, W_ = like.shape
        return t.transpose(0, 2, 1).reshape(B_, C_, H_, W_)
    x = _L0_conv_ref(x, L0_conv_w1, L0_conv_b1, L0_conv_w2, L0_conv_b2)
    x = _L1_conv_ref(x, L1_conv_qkv_w, L1_conv_o1_w, L1_conv_o2_w, L1_conv_kln_w, L1_conv_kln_b, L1_conv_vln_w, L1_conv_vln_b)
    return x

_drawn_inputs = setup_inputs


def setup_inputs(seed=0):
    import zlib

    import numpy as np

    out = dict(_drawn_inputs(seed))
    spreads = {}
    factors = {'L0_conv_b1': 8.0, 'L0_conv_b2': 8.0}
    for name, (base, spread) in spreads.items():
        noise = np.random.default_rng([zlib.crc32(name.encode()), seed]).standard_normal(out[name].shape)
        drawn = base * np.exp(spread * noise) if base else spread * noise
        out[name] = jnp.asarray(drawn.astype(out[name].dtype))
    for name, factor in factors.items():
        out[name] = (out[name] * factor).astype(out[name].dtype)
    return out
```

```python
import concourse.bass as bass
from concourse import mybir
from contextlib import ExitStack

F32 = mybir.dt.float32
F32R = mybir.dt.float32r
ALU = mybir.AluOpType
ACT = mybir.ActivationFunctionType
AX = mybir.AxisListType

IMAGES, CH, ROWS, COLS = 16, 64, 64, 64
P = 2 * CH
PAIRS = IMAGES // 2
GROUPS = ROWS // 2
SKEWED = GROUPS + 1
PIX = GROUPS * COLS
STEPS = 3
H_STEP = 1.0 / 3.0
K = 3
PADDED = COLS + 2
BANK = 512

HEADS, HD = 8, 8
KV = 2 * CH
LN_EPS = 1e-5
ONE = CH + 1
BLOCKS = PIX // P
PER_BANK = BANK // (2 * KV)
PROJ = BLOCKS // PER_BANK
PX_BANK = 2 * PER_BANK
TAILS = PIX // BANK

SIZES = ((7, 7, 7, 6, 6), (8, 8, 8, 8))
SLOTS = [(k, k % 2, (k // 2) % 2, k // 4) for k in range(4 * STEPS)]
CHUNKS = [(slot, img, conv, step, sum(SIZES[conv][:n]), size)
          for slot, img, conv, step in SLOTS for n, size in enumerate(SIZES[conv])]
NC = len(CHUNKS)
SLOT_END = [sum(c[0] <= slot for c in CHUNKS) for slot in range(len(SLOTS))]
CONV_BANKS = 3
RING = 4
assert NC % CONV_BANKS == 0
X_SPLIT = {46: (0, 0), 47: (0, 1), 48: (1, 0), 49: (1, 1)}

SCHEDULE = [[] for _ in range(NC)]
for _img, _at in ((0, 0), (1, 14)):
    for _b in range(PROJ):
        SCHEDULE[_at + _b].append(("project", _img, _b))
    SCHEDULE[_at + 8].append(("deviation", _img, 0))
    for _b in range(PROJ):
        SCHEDULE[_at + 9 + _b // 2].append(("normalise", _img, _b))
    for _b in range(PROJ):
        SCHEDULE[_at + 10 + _b // 2].append(("outer", _img, _b))
    for _k in range(4):
        SCHEDULE[_at + 14 + _k].append(("fold", _img, _k))
for _img, _at in ((0, 27), (1, 33)):
    for _c in range(TAILS):
        SCHEDULE[_at + _c].append(("up", _img, _c))
    for _c in range(TAILS):
        SCHEDULE[_at + 1 + _c].append(("down", _img, _c))
RING_USES = [s for gap in SCHEDULE for s in gap if s[0] in ("project", "up", "down")]
assert len(RING_USES) % RING == 0


def conv_attention_kernel(nc, x, w1, b1, w2, b2, qkv_w, o1_w, o2_w, kln_w, kln_b, vln_w, vln_b, out):
    x_v = x.rearrange("(i k) c (j p) w -> i k p c j w", k=2, p=2)
    out_v = out.rearrange("(i k) c (j p) w -> i k p c j w", k=2, p=2)

    ctx = ExitStack()
    with ctx:
        def sb(name, shape, dt=F32):
            return ctx.enter_context(nc.sbuf_tensor(name, shape, dt))

        def sem(name):
            return ctx.enter_context(nc.semaphore(name))

        def pair_of(name, shape, dt=F32):
            return [sb(f"{name}{k}", shape, dt) for k in range(2)]

        x_in = pair_of("x_in", [P, GROUPS, COLS])
        x_res = pair_of("x_res", [P, GROUPS, COLS])
        x_hi = pair_of("x_hi", [P, GROUPS + 2, PADDED], F32R)
        x_lo = pair_of("x_lo", [P, GROUPS + 2, PADDED], F32R)
        t_hi = pair_of("t_hi", [P, SKEWED, PADDED], F32R)
        t_lo = pair_of("t_lo", [P, SKEWED, PADDED], F32R)
        drain = [sb(f"drain{k}", [P, BANK]) for k in range(CONV_BANKS)]
        f = pair_of("f", [P, PIX])
        f_hi = pair_of("f_hi", [P, PIX], F32R)
        f_lo = pair_of("f_lo", [P, PIX], F32R)
        kv = sb("kv", [P, BLOCKS * 2 * 2, ONE])
        squares = pair_of("squares", [P, BANK])
        variance = sb("variance", [P, PROJ, BANK // HD])
        rstd = sb("rstd", [P, PROJ, BANK // HD])
        g = pair_of("g", [P, BANK])
        g_hi = pair_of("g_hi", [P, BANK], F32R)
        g_lo = pair_of("g_lo", [P, BANK], F32R)
        y = [sb(f"y{k}", [P, BANK]) for k in range(4)]
        w_hi = sb("w_hi", [P, 2 * 2 * K, P], F32R)
        w_lo = sb("w_lo", [P, 2 * 2 * K, P], F32R)
        kvw_hi = sb("kvw_hi", [P, 2 * KV], F32R)
        kvw_lo = sb("kvw_lo", [P, 2 * KV], F32R)
        gw_hi = sb("gw_hi", [P, P], F32R)
        gw_lo = sb("gw_lo", [P, P], F32R)
        o2_hi = sb("o2_hi", [P, P], F32R)
        o2_lo = sb("o2_lo", [P, P], F32R)
        b1_col = sb("b1_col", [P, 1])
        b2_col = sb("b2_col", [P, 1])
        b2_third = sb("b2_third", [P, 1])
        ident = sb("ident", [P, P])
        ident2 = sb("ident2", [CH, 2, CH])
        head_mask = sb("head_mask", [CH, HEADS, HD])
        k_affine = sb("k_affine", [ONE, CH])
        v_affine = sb("v_affine", [ONE, CH])
        ln_cols = sb("ln_cols", [CH, 2])
        q_w = sb("q_w", [ONE, CH])
        o1_t = sb("o1_t", [CH, CH])
        outer_sb = sb("outer_sb", [ONE, ONE])
        half_affine = sb("half_affine", [ONE, CH])
        kv_head = sb("kv_head", [ONE, CH])
        mix = sb("mix", [CH, 2, CH])
        w_raw = [f[k][0:CH, 0:CH * K * K] for k in range(2)]
        w_taps = [f[k][0:CH, 1024:1024 + K * (K + 2) * CH].rearrange("o (x s c) -> o x s c", x=K, s=K + 2)
                  for k in range(2)]
        kv_rows = squares[0][:, 0:CH]
        kv_rows2 = squares[0][:, 0:2 * CH].rearrange("o (r c) -> o r c", r=2)
        o_rows = squares[1][0:CH, 0:2 * CH].rearrange("o (r c) -> o r c", r=2)
        o1_rows = squares[1][0:CH, 2 * CH:3 * CH]
        kvw_sum = g[0][:, 0:KV // HD]
        kvw_mean = g[0][:, 64:64 + KV // HD]
        kvw_centred = g[1][:, 0:KV]

        banks = [ctx.enter_context(nc.psum_tensor(f"bank{k}", [P, BANK], F32)) for k in range(8)]
        conv_ps = banks[0:CONV_BANKS]
        ring_ps = banks[CONV_BANKS:CONV_BANKS + RING]
        small_ps = banks[7]
        outer_ps = small_ps[0:ONE, 0:ONE]
        half_ps = small_ps[0:ONE, 128:128 + CH]
        head_ps = small_ps[0:CH, 192:192 + CH]
        mix_ps = small_ps[0:CH, 256:256 + CH]
        gw_ps = small_ps[:, 320:320 + CH]

        weights_in = sem("weights_in")
        zeroed = sem("zeroed")
        consts_made = sem("consts_made")
        taps_ready = sem("taps_ready")
        transposed = sem("transposed")
        setup_step = sem("setup_step")
        setup_done = sem("setup_done")
        conv_ready = sem("conv_ready")
        drained = sem("drained")
        edge_cleared = sem("edge_cleared")
        residual_added = sem("residual_added")
        final_relu = sem("final_relu")
        hi_written = sem("hi_written")
        conv_out = sem("conv_out")
        x_loaded = [sem(f"x_loaded{k}") for k in range(2)]
        x_hi_split = sem("x_hi_split")
        x_split = sem("x_split")
        proj_ready = sem("proj_ready")
        proj_taken = sem("proj_taken")
        squares_summed = sem("squares_summed")
        std_ready = sem("std_ready")
        std_eps = sem("std_eps")
        rstd_ready = sem("rstd_ready")
        normalised = sem("normalised")
        small_ready = sem("small_ready")
        gw_hi_written = sem("gw_hi_written")
        small_taken = sem("small_taken")
        up_ready = sem("up_ready")
        gelu_done = sem("gelu_done")
        g_hi_written = sem("g_hi_written")
        g_split = sem("g_split")
        down_ready = sem("down_ready")
        down_added = sem("down_added")
        y_ready = sem("y_ready")
        stored = [sem(f"stored{k}") for k in range(4)]

        block = ctx.enter_context(nc.Block())
        WEIGHT_DMAS = 2 + 4 + 3 * HEADS + 3 + 4

        @block.sync
        def _(sp):
            for k in range(2):
                for p in range(2):
                    sp.dma_start(x_in[k][CH * p:CH * p + CH, :, :], x_v[0, k, p]).then_inc(x_loaded[k], 16)
            for k in range(4):
                sp.sem_inc(stored[k], 32)

            def load(i, k):
                sp.wait_ge(conv_out, i * NC + SLOT_END[2 + k])
                for p in range(2):
                    sp.dma_start(x_in[k][CH * p:CH * p + CH, :, :], x_v[i + 1, k, p]).then_inc(x_loaded[k], 16)

            def store(a, k, c):
                sp.wait_ge(y_ready, a * 2 * TAILS + k * TAILS + c + 1)
                for p in range(2):
                    sp.dma_start(out_v[a, k, p][:, c * 8:c * 8 + 8, :],
                                 y[c][CH * p:CH * p + CH, :].rearrange("c (j w) -> c j w", w=COLS)
                                 ).then_inc(stored[c], 16)

            def iteration(i, loads, stores):
                if loads:
                    load(i, 0)
                    load(i, 1)
                if stores:
                    for k in range(2):
                        for c in range(TAILS):
                            store(i - 1, k, c)

            iteration(0, True, False)
            with sp.Fori(1, PAIRS - 1) as i:
                iteration(i, True, True)
            iteration(PAIRS - 1, False, True)
            iteration(PAIRS, False, True)
            for k in range(4):
                sp.wait_ge(stored[k], 32 * (1 + IMAGES))

        @block.gpsimd
        def _(pool):
            nc.gpsimd.memset(ident[:, :], 0.0).then_inc(zeroed, 1)
            nc.gpsimd.memset(head_mask[:, :, :], 1.0 / (ROWS * COLS)).then_inc(zeroed, 1)
            pool.wait_ge(zeroed, 2)
            nc.gpsimd.affine_select(out=ident[:, :], in_=ident[:, :], compare_op=ALU.not_equal, fill=1.0,
                                    base=0, pattern=[[-1, P]], channel_multiplier=1).then_inc(consts_made, 1)
            nc.gpsimd.affine_select(out=head_mask[:, :, :], in_=head_mask[:, :, :], compare_op=ALU.is_ge, fill=0.0,
                                    base=0, pattern=[[-HD, HEADS], [0, HD]], channel_multiplier=1).then_inc(zeroed, 1)
            pool.wait_ge(zeroed, 3)
            nc.gpsimd.affine_select(out=head_mask[:, :, :], in_=head_mask[:, :, :], compare_op=ALU.is_ge, fill=0.0,
                                    base=HD - 1, pattern=[[HD, HEADS], [0, HD]], channel_multiplier=-1
                                    ).then_inc(consts_made, 1)
            for k in range(2):
                for t in (t_hi, t_lo):
                    nc.gpsimd.memset(t[k][:, :, :].bitcast(F32), 0.0).then_inc(consts_made, 1)
            nc.gpsimd.memset(kv[:, :, CH:ONE], 1.0).then_inc(consts_made, 1)

        @block.scalar
        def _(act):
            for k, w in enumerate((w1, w2)):
                act.dma_start(w_raw[k], w.rearrange("o c y x -> o (c y x)")).then_inc(weights_in, 16)
            for p in range(2):
                act.dma_start(b1_col[CH * p:CH * p + CH, :], b1.rearrange("(c a) -> c a", a=1)).then_inc(weights_in, 16)
                act.dma_start(b2_col[CH * p:CH * p + CH, :], b2.rearrange("(c a) -> c a", a=1)).then_inc(weights_in, 16)
            qkv_v = qkv_w.rearrange("(h t d) c -> h t d c", h=HEADS, t=3)
            for h in range(HEADS):
                for t, (rows, at) in enumerate(((q_w, 0), (kv_rows, 0), (kv_rows, CH))):
                    act.dma_start(rows[at + HD * h:at + HD * (h + 1), :], qkv_v[h, t]).then_inc(weights_in, 16)
            act.dma_start(o1_rows, o1_w).then_inc(weights_in, 16)
            for r in range(2):
                act.dma_start(o_rows[:, r, :], o2_w).then_inc(weights_in, 16)
            for k, (w, b, mat) in enumerate(((kln_w, kln_b, k_affine), (vln_w, vln_b, v_affine))):
                act.dma_start(ln_cols[:, k:k + 1], w.rearrange("h a d -> (h d) a")).then_inc(weights_in, 16)
                act.dma_start(mat[CH:ONE, :], b.rearrange("h a d -> a (h d)")).then_inc(weights_in, 16)

            act.wait_ge(setup_done, 1)

            def drain_conv(i, n):
                slot, img, conv, step, g0, size = CHUNKS[n]
                act.wait_ge(conv_ready, i * NC + n + 1)
                if not (isinstance(i, int) and i == 0 and n < CONV_BANKS):
                    act.wait_ge(conv_out, i * NC + n - CONV_BANKS + 1)
                to, at = drain[n % CONV_BANKS][:, 0:size * COLS], conv_ps[n % CONV_BANKS][:, 0:size * COLS]
                if conv == 0:
                    nc.scalar.activation(to, at, ACT.Relu, bias=b1_col[:, :]).then_inc(drained, 1)
                else:
                    nc.scalar.activation(to, at, ACT.Identity, bias=b2_third[:, :], scale=H_STEP).then_inc(drained, 1)

            ring = {s: r % RING for r, s in enumerate(RING_USES)}

            def attention(a, n):
                for s in SCHEDULE[n]:
                    kind, img, k = s
                    if kind == "project":
                        done = a * 2 * PROJ + img * PROJ + k
                        act.wait_ge(proj_ready, done + 1)
                        if img and k == 0:
                            act.wait_ge(small_ready, a * 10 + 1)
                        ps = ring_ps[ring[s]]
                        nc.scalar.activation(kv[:, 2 * PX_BANK * k:2 * PX_BANK * (k + 1), 0:CH],
                                             ps[:, :].rearrange("p (g c) -> p g c", c=CH), ACT.Copy)
                        if img or k >= 2:
                            act.wait_ge(squares_summed, done - 1)
                        nc.scalar.activation(squares[k % 2][:, :], ps[:, :], ACT.Square).then_inc(proj_taken, 1)
                    elif kind == "deviation":
                        act.wait_ge(squares_summed, a * 2 * PROJ + (img + 1) * PROJ)
                        nc.scalar.activation(rstd[:, :, :], variance[:, :, :], ACT.Sqrt,
                                             scale=1.0 / (HD - 1)).then_inc(std_ready, 1)
                    elif kind == "up":
                        done = a * 2 * TAILS + img * TAILS + k
                        act.wait_ge(up_ready, done + 1)
                        if img or k >= 2:
                            act.wait_ge(g_split, done - 1)
                        nc.scalar.activation(g[k % 2][:, :], ring_ps[ring[s]][:, :], ACT.Gelu).then_inc(gelu_done, 1)
                    elif kind == "down":
                        act.wait_ge(down_added, a * 2 * TAILS + img * TAILS + k + 1)
                        nc.scalar.activation(y[k][:, :], y[k][:, :], ACT.Gelu).then_inc(y_ready, 1)

            def iteration(i, convs, attends):
                for n in range(NC):
                    if convs:
                        drain_conv(i, n)
                    if attends:
                        attention(i - 1, n)

            iteration(0, True, False)
            with act.Fori(1, PAIRS - 1) as i:
                iteration(i, True, True)
            iteration(PAIRS - 1, True, True)
            iteration(PAIRS, False, True)

        @block.vector
        def _(dve):
            v = nc.vector
            steps = 0

            def link(instruction):
                nonlocal steps
                steps += 1
                instruction.then_inc(setup_step, 1)
                dve.wait_ge(setup_step, steps)

            for k in range(2):
                v.memset(x_hi[k][:, :, :].bitcast(F32), 0.0)
                v.memset(x_lo[k][:, :, :].bitcast(F32), 0.0)
            v.memset(kvw_hi[:, :].bitcast(F32), 0.0)
            v.memset(kvw_lo[:, :].bitcast(F32), 0.0)
            v.memset(gw_hi[:, :].bitcast(F32), 0.0)
            v.memset(gw_lo[:, :].bitcast(F32), 0.0)
            v.memset(o2_hi[:, :].bitcast(F32), 0.0)
            v.memset(kv_head[CH:ONE, :], 0.0)
            v.memset(q_w[CH:ONE, :], 0.0)
            for k in range(2):
                v.memset(w_taps[k][:, :, 0, :], 0.0)
                v.memset(w_taps[k][:, :, K + 1, :], 0.0)
            link(v.memset(o2_lo[:, :].bitcast(F32), 0.0))
            dve.wait_ge(weights_in, 16 * WEIGHT_DMAS)
            for k in range(2):
                raw = w_raw[k].rearrange("o (c y x) -> o y x c", y=K, x=K)
                for r in range(K):
                    v.tensor_copy(w_taps[k][:, :, 1 + r, :], raw[:, r if k == 0 else K - 1 - r, :, :])
            link(v.tensor_copy(kv_rows2[:, 1, :], kv_rows2[:, 0, :]))
            v.tensor_scalar(b2_third[:, :], b2_col[:, :], H_STEP, None, ALU.mult)
            dve.wait_ge(consts_made, 2)
            v.tensor_copy(ident2[:, 0, :], ident[0:CH, 0:CH])
            v.tensor_copy(ident2[:, 1, :], ident[0:CH, 0:CH])
            v.tensor_scalar(k_affine[0:CH, :], ident[0:CH, 0:CH], ln_cols[:, 0:1], None, ALU.mult)
            v.tensor_scalar(v_affine[0:CH, :], ident[0:CH, 0:CH], ln_cols[:, 1:2], None, ALU.mult
                            ).then_inc(taps_ready, 1)

            def split_setup(hi, lo, value):
                link(v.tensor_copy(hi, value))
                v.tensor_tensor(lo, value, hi.bitcast(F32), ALU.subtract)

            dve.wait_ge(transposed, 1)
            for k in range(2):
                for xx in range(K):
                    for half in range(2):
                        at = (k * 2 + (half if k == 0 else 1 - half)) * K + xx
                        split_setup(w_hi[:, at, :], w_lo[:, at, :], banks[k * K + xx][:, half * P:half * P + P])
            heads = banks[6][:, 0:KV].rearrange("p (h d) -> p h d", d=HD)
            link(v.tensor_reduce(kvw_sum, heads, AX.X, ALU.add))
            link(v.tensor_scalar(kvw_mean, kvw_sum, 1.0 / HD, None, ALU.mult))
            link(v.tensor_tensor(kvw_centred.rearrange("p (h d) -> p h d", d=HD), heads,
                                 kvw_mean.rearrange("p (h a) -> p h a", a=1).broadcast_to([P, KV // HD, HD]),
                                 ALU.subtract))
            for p in range(2):
                rows = slice(CH * p, CH * p + CH)
                split_setup(kvw_hi[rows, KV * p:KV * p + KV], kvw_lo[rows, KV * p:KV * p + KV], kvw_centred[rows, :])
                split_setup(o2_hi[rows, CH * p:CH * p + CH], o2_lo[rows, CH * p:CH * p + CH], banks[7][rows, 0:CH])
            link(v.tensor_copy(o1_t[:, :], banks[7][0:CH, CH:2 * CH]))

            def split_x(i, k, half):
                groups = slice(16 * half, 16 * half + 16)
                inner = slice(16 * half + 1, 16 * half + 17)
                dve.wait_ge(x_loaded[k], 32 * (i + 1))
                v.tensor_copy(x_hi[k][:, inner, 1:COLS + 1], x_in[k][:, groups, :]).then_inc(x_hi_split, 1)
                dve.wait_ge(x_hi_split, i * 4 + 2 * k + half + 1)
                v.tensor_tensor(x_lo[k][:, inner, 1:COLS + 1], x_in[k][:, groups, :],
                                x_hi[k][:, inner, 1:COLS + 1].bitcast(F32), ALU.subtract).then_inc(x_split, 1)

            for k in range(2):
                for half in range(2):
                    split_x(0, k, half)
            dve.wait_ge(consts_made, 7)
            v.memset(kvw_sum, 0.0).then_inc(setup_done, 1)

            def take_conv(i, n):
                slot, img, conv, step, g0, size = CHUNKS[n]
                dve.wait_ge(drained, i * NC + n + 1)
                value = drain[n % CONV_BANKS][:, 0:size * COLS].rearrange("p (j w) -> p j w", w=COLS)
                if conv == 0:
                    hi, lo = (t[img][:, g0:g0 + size, 1:COLS + 1] for t in (t_hi, t_lo))
                    before = 2 * sum(c[2] == 0 for c in SLOTS[:slot])
                    c1_slots = 2 * sum(c[2] == 0 for c in SLOTS)
                    if g0 == 0:
                        v.memset(value[CH:P, 0, :], 0.0).then_inc(edge_cleared, 1)
                        dve.wait_ge(edge_cleared, i * c1_slots + before + 1)
                    if g0 + size == SKEWED:
                        v.memset(value[0:CH, size - 1, :], 0.0).then_inc(edge_cleared, 1)
                        dve.wait_ge(edge_cleared, i * c1_slots + before + 2)
                else:
                    before = sum(c[2] for c in CHUNKS[:n])
                    groups = slice(g0, g0 + size)
                    pixels = slice(g0 * COLS, (g0 + size) * COLS)
                    source = (x_in if step == 0 else x_res)[img][:, groups, :]
                    total = x_res[img][:, groups, :] if step < STEPS - 1 else value
                    v.tensor_tensor(total, value, source, ALU.add).then_inc(residual_added, 1)
                    dve.wait_ge(residual_added, i * sum(c[2] for c in CHUNKS) + before + 1)
                    value = total
                    if step == STEPS - 1:
                        value = f[img][:, pixels]
                        v.tensor_scalar(value, drain[n % CONV_BANKS][:, :], 0.0, None, ALU.max).then_inc(final_relu, 1)
                        dve.wait_ge(final_relu, i * 2 * TAILS + img * TAILS + g0 // size + 1)
                        hi, lo = f_hi[img][:, pixels], f_lo[img][:, pixels]
                    else:
                        hi, lo = (t[img][:, g0 + 1:g0 + 1 + size, 1:COLS + 1] for t in (x_hi, x_lo))
                v.tensor_copy(hi, value).then_inc(hi_written, 1)
                dve.wait_ge(hi_written, i * NC + n + 1)
                v.tensor_tensor(lo, value, hi.bitcast(F32), ALU.subtract).then_inc(conv_out, 1)

            ring = {s: r % RING for r, s in enumerate(RING_USES)}

            def attention(a, n):
                for s in SCHEDULE[n]:
                    kind, img, k = s
                    bank = a * 2 * PROJ + img * PROJ + k
                    tail = a * 2 * TAILS + img * TAILS + k
                    if kind == "project":
                        dve.wait_ge(proj_taken, bank + 1)
                        v.tensor_reduce(variance[:, k, :], squares[k % 2][:, :].rearrange("p (h d) -> p h d", d=HD),
                                        AX.X, ALU.add).then_inc(squares_summed, 1)
                    elif kind == "deviation":
                        dve.wait_ge(std_ready, a * 2 + img + 1)
                        v.tensor_scalar(rstd[:, :, :], rstd[:, :, :], LN_EPS, None, ALU.add).then_inc(std_eps, 1)
                        dve.wait_ge(std_eps, a * 2 + img + 1)
                        v.reciprocal(rstd[:, :, :], rstd[:, :, :]).then_inc(rstd_ready, 1)
                        dve.wait_ge(rstd_ready, a * 2 + img + 1)
                    elif kind == "normalise":
                        rows = kv[:, 2 * PX_BANK * k:2 * PX_BANK * (k + 1), 0:CH].rearrange("p g (h d) -> p g h d", d=HD)
                        scale = rstd[:, k, :].rearrange("p (g h a) -> p g h a", h=HEADS, a=1)
                        v.tensor_tensor(rows, rows, scale.broadcast_to([P, 2 * PX_BANK, HEADS, HD]), ALU.mult
                                        ).then_inc(normalised, 1)
                    elif kind == "outer" and k == PROJ - 1:
                        dve.wait_ge(small_ready, a * 10 + img * 5 + 1)
                        v.tensor_copy(outer_sb[:, :], outer_ps).then_inc(small_taken, 1)
                    elif kind == "fold":
                        dve.wait_ge(small_ready, a * 10 + img * 5 + k + 2)
                        if k == 0:
                            v.tensor_copy(half_affine[:, :], half_ps).then_inc(small_taken, 1)
                        elif k == 1:
                            v.tensor_tensor(kv_head[0:CH, :], head_ps, head_mask[:, :, :].rearrange("p h d -> p (h d)"),
                                            ALU.mult).then_inc(small_taken, 1)
                        elif k == 2:
                            v.tensor_tensor(mix[:, 0, :], mix_ps, ident2[:, 0, :], ALU.add)
                            v.tensor_tensor(mix[:, 1, :], mix_ps, ident2[:, 1, :], ALU.add).then_inc(small_taken, 1)
                        else:
                            for p in range(2):
                                rows, cols = slice(CH * p, CH * p + CH), slice(CH * p, CH * p + CH)
                                v.tensor_copy(gw_hi[rows, cols], gw_ps[rows, :]).then_inc(gw_hi_written, 1)
                                dve.wait_ge(gw_hi_written, a * 4 + img * 2 + p + 1)
                                low = v.tensor_tensor(gw_lo[rows, cols], gw_ps[rows, :],
                                                      gw_hi[rows, cols].bitcast(F32), ALU.subtract)
                            low.then_inc(small_taken, 1)
                    elif kind == "up":
                        dve.wait_ge(gelu_done, tail + 1)
                        if img or k >= 2:
                            dve.wait_ge(down_ready, tail - 1)
                        v.tensor_copy(g_hi[k % 2][:, :], g[k % 2][:, :]).then_inc(g_hi_written, 1)
                        dve.wait_ge(g_hi_written, tail + 1)
                        v.tensor_tensor(g_lo[k % 2][:, :], g[k % 2][:, :], g_hi[k % 2][:, :].bitcast(F32),
                                        ALU.subtract).then_inc(g_split, 1)
                    elif kind == "down":
                        dve.wait_ge(down_ready, tail + 1)
                        dve.wait_ge(stored[k], 32 * (a * 2 + img + 1))
                        v.tensor_tensor(y[k][:, :], ring_ps[ring[s]][:, :], f[img][:, BANK * k:BANK * (k + 1)],
                                        ALU.add).then_inc(down_added, 1)

            def iteration(i, convs, attends, splits):
                for n in range(NC):
                    if convs:
                        take_conv(i, n)
                    if attends:
                        attention(i - 1, n)
                    if splits and n in X_SPLIT:
                        split_x(i + 1, *X_SPLIT[n])

            iteration(0, True, False, True)
            with dve.Fori(1, PAIRS - 1) as i:
                iteration(i, True, True, True)
            iteration(PAIRS - 1, True, True, False)
            iteration(PAIRS, False, True, False)

        @block.tensor
        def _(pe):
            mm = nc.tensor.matmul
            pe.wait_ge(taps_ready, 1)
            for k in range(2):
                for xx in range(K):
                    for q in range(4):
                        nc.tensor.transpose(banks[k * K + xx][:, q * CH:q * CH + CH],
                                            w_taps[k][:, xx, q:q + 2, :].rearrange("o s c -> o (s c)"),
                                            ident[0:CH, 0:CH])
            nc.tensor.transpose(banks[6][:, 0:KV], kv_rows2.rearrange("o r c -> o (r c)"), ident[:, :])
            nc.tensor.transpose(banks[7][:, 0:CH], o_rows.rearrange("o r c -> o (r c)"), ident[0:CH, 0:CH])
            nc.tensor.transpose(banks[7][0:CH, CH:2 * CH], o1_rows, ident[0:CH, 0:CH]).then_inc(transposed, 1)
            pe.wait_ge(setup_done, 1)

            def three(ps, lhs, rhs, first, last):
                mm(ps, lhs[0], rhs[0], start=first, stop=False)
                mm(ps, lhs[1], rhs[0], start=False, stop=False)
                return mm(ps, lhs[0], rhs[1], start=False, stop=last)

            def convolve(i, n):
                slot, img, conv, step, g0, size = CHUNKS[n]
                if g0 == 0:
                    if slot < 2:
                        pe.wait_ge(x_split, i * 4 + 2 * slot + 2)
                    else:
                        pe.wait_ge(conv_out, i * NC + SLOT_END[slot - 2])
                if not (isinstance(i, int) and i == 0 and n < CONV_BANKS):
                    pe.wait_ge(drained, i * NC + n - CONV_BANKS + 1)
                hi, lo = (x_hi, x_lo) if conv == 0 else (t_hi, t_lo)
                ps = conv_ps[n % CONV_BANKS][:, 0:size * COLS]
                for stack in range(2):
                    for xx in range(K):
                        at = (conv * 2 + stack) * K + xx
                        groups, cols = slice(g0 + stack, g0 + stack + size), slice(xx, xx + COLS)
                        last = three(ps, (w_hi[:, at, :], w_lo[:, at, :]),
                                     (hi[img][:, groups, cols], lo[img][:, groups, cols]),
                                     stack == 0 and xx == 0, stack == 1 and xx == K - 1)
                last.then_inc(conv_ready, 1)

            ring = {s: r for r, s in enumerate(RING_USES)}

            def ring_free(a, s):
                r = ring[s]
                if r >= RING:
                    kind, img, k = RING_USES[r - RING]
                    if kind == "project":
                        pe.wait_ge(proj_taken, a * 2 * PROJ + img * PROJ + k + 1)
                    elif kind == "up":
                        pe.wait_ge(gelu_done, a * 2 * TAILS + img * TAILS + k + 1)
                    else:
                        pe.wait_ge(down_added, a * 2 * TAILS + img * TAILS + k + 1)
                return ring_ps[r % RING]

            def attention(a, n):
                for s in SCHEDULE[n]:
                    kind, img, k = s
                    tail = a * 2 * TAILS + img * TAILS + k
                    if kind == "project":
                        if k == 0:
                            pe.wait_ge(conv_out, (a + 1) * NC - (0 if img else TAILS))
                        ps = ring_free(a, s)
                        for j in range(PER_BANK):
                            at = slice(P * (PER_BANK * k + j), P * (PER_BANK * k + j + 1))
                            to = ps[:, 2 * KV * j:2 * KV * (j + 1)]
                            mm(to, f_hi[img][:, at], kvw_hi[:, :], start=True, stop=False)
                            mm(to, f_hi[img][:, at], kvw_lo[:, :], start=False, stop=False)
                            last = mm(to, f_lo[img][:, at], kvw_hi[:, :], start=False, stop=True)
                        last.then_inc(proj_ready, 1)
                    elif kind == "outer":
                        pe.wait_ge(normalised, a * 2 * PROJ + img * PROJ + k + 1)
                        if img and k == 0:
                            pe.wait_ge(small_taken, a * 10 + 5)
                        for j in range(PX_BANK):
                            at = 2 * (PX_BANK * k + j)
                            last = mm(outer_ps, kv[:, at, :], kv[:, at + 1, :], start=(k == 0 and j == 0),
                                      stop=(k == PROJ - 1 and j == PX_BANK - 1))
                        if k == PROJ - 1:
                            last.then_inc(small_ready, 1)
                    elif kind == "fold":
                        pe.wait_ge(small_taken, a * 10 + img * 5 + k + 1)
                        if k == 0:
                            last = mm(half_ps, outer_sb[:, :], k_affine[:, :], start=True, stop=True)
                        elif k == 1:
                            last = mm(head_ps, half_affine[:, :], v_affine[:, :], start=True, stop=True)
                        elif k == 2:
                            last = mm(mix_ps, kv_head[:, :], q_w[:, :], start=True, stop=True)
                        else:
                            last = mm(gw_ps, mix[:, :, :].rearrange("p r c -> p (r c)"), o1_t[:, :],
                                      start=True, stop=True)
                        last.then_inc(small_ready, 1)
                    elif kind == "up":
                        if k == 0:
                            pe.wait_ge(small_taken, a * 10 + img * 5 + 5)
                        at = slice(BANK * k, BANK * (k + 1))
                        three(ring_free(a, s)[:, :], (gw_hi[:, :], gw_lo[:, :]), (f_hi[img][:, at], f_lo[img][:, at]),
                              True, True).then_inc(up_ready, 1)
                    elif kind == "down":
                        pe.wait_ge(g_split, tail + 1)
                        three(ring_free(a, s)[:, :], (o2_hi[:, :], o2_lo[:, :]), (g_hi[k % 2][:, :], g_lo[k % 2][:, :]),
                              True, True).then_inc(down_ready, 1)

            def iteration(i, convs, attends):
                for n in range(NC):
                    if convs:
                        convolve(i, n)
                    if attends:
                        attention(i - 1, n)

            iteration(0, True, False)
            with pe.Fori(1, PAIRS - 1) as i:
                iteration(i, True, True)
            iteration(PAIRS - 1, True, True)
            iteration(PAIRS, False, True)


_INS = ["x", "L0_conv_w1", "L0_conv_b1", "L0_conv_w2", "L0_conv_b2", "L1_conv_qkv_w", "L1_conv_o1_w", "L1_conv_o2_w",
        "L1_conv_kln_w", "L1_conv_kln_b", "L1_conv_vln_w", "L1_conv_vln_b"]


def kernel(**inputs):
    import numpy as np
    import concourse.bacc as bacc
    from concourse.bass_utils import run_bass_kernel_spmd

    nc = bacc.Bacc("TRN2", target_bir_lowering=False, num_devices=1, dynamic_dma_scratch_size=1024)
    arrays, args = {}, []
    for name in _INS:
        a = np.ascontiguousarray(inputs[name])
        arrays[f"in_{name}"] = a
        args.append(nc.dram_tensor(f"in_{name}", a.shape, mybir.dt.from_np(a.dtype), kind="ExternalInput").ap())
    args.append(nc.dram_tensor("out", (IMAGES, CH, ROWS, COLS), F32, kind="ExternalOutput").ap())
    conv_attention_kernel(nc, *args)
    r = run_bass_kernel_spmd(nc, [arrays], core_ids=[0])
    return r.results[0]["out"]
```

```python
import concourse.bass as bass
from concourse import mybir
from contextlib import ExitStack

F32 = mybir.dt.float32
F32R = mybir.dt.float32r
ALU = mybir.AluOpType
ACT = mybir.ActivationFunctionType
AX = mybir.AxisListType

IMAGES, CH, ROWS, COLS = 16, 64, 64, 64
P = 2 * CH
PAIRS = IMAGES // 2
GROUPS = ROWS // 2
SKEWED = GROUPS + 1
PIX = GROUPS * COLS
STEPS = 3
H_STEP = 1.0 / 3.0
K = 3
PADDED = COLS + 2
BANK = 512

HEADS, HD = 8, 8
KV = 2 * CH
LN_EPS = 1e-5
ONE = CH + 1
BLOCKS = PIX // P
PER_BANK = BANK // (2 * KV)
PROJ = BLOCKS // PER_BANK
PX_BANK = 2 * PER_BANK
TAILS = PIX // BANK

SIZES = ((7, 7, 7, 6, 6), (8, 8, 8, 8))
SLOTS = [(k, k % 2, (k // 2) % 2, k // 4) for k in range(4 * STEPS)]
CHUNKS = [(slot, img, conv, step, sum(SIZES[conv][:n]), size)
          for slot, img, conv, step in SLOTS for n, size in enumerate(SIZES[conv])]
NC = len(CHUNKS)
SLOT_END = [sum(c[0] <= slot for c in CHUNKS) for slot in range(len(SLOTS))]
CONV_BANKS = 3
RING = 4
QUARTERS = 4
HALF = COLS // 2


def winograd(n):
    return CHUNKS[n][1] == 1 and CHUNKS[n][2] == 1




def made_by_dve(n):
    return CHUNKS[n % NC][1] == 1 or CHUNKS[n % NC][2] == 1


VALUES = sum(made_by_dve(n) for n in range(NC))


def value_number(n):
    return sum(made_by_dve(m) for m in range(n % NC + 1)) + n // NC * VALUES


def combined_number(n):
    return sum(c[0] == CHUNKS[n][0] for c in CHUNKS[:n]) % 2


UNITS = [1 + winograd(n) for n in range(NC)]
UNIT = [sum(UNITS[:n]) for n in range(NC)]
NU = sum(UNITS)
assert NU % CONV_BANKS == 0
DRAINS = 4


def last_use(n):
    mine = {(UNIT[n] + k) % DRAINS for k in range(UNITS[n])}
    before = [(m, UNIT[m % NC], UNITS[m % NC]) for m in range(n - NC, n)]
    return max(m for m, unit, units in before if mine & {(unit + k) % DRAINS for k in range(units)})


X_SPLIT = {42: (0, 0), 44: (0, 1), 46: (1, 0), 48: (1, 1)}

PROJECT, DEVIATION, INVERT, NORMALISE, OUTER, FOLD, UP, DOWN = (
    "project", "deviation", "invert", "normalise", "outer", "fold", "up", "down")


def steps(kind, img, *numbers):
    return [(kind, img, k) for k in numbers]


LATE = {n: [] for n in range(NC)}
for _kind, _img, _gaps in (
        (PROJECT, 0, (0, 0, 1, 1, 2, 2, 3, 3)), (DEVIATION, 0, (3, 5)), (INVERT, 0, (4, 6)),
        (NORMALISE, 0, (7, 9, 10, 10, 11, 11, 12, 12)), (OUTER, 0, (9, 10, 11, 11, 12, 12, 13, 13)),
        (FOLD, 0, (16, 18, 20, 22)),
        (PROJECT, 1, (14, 15, 18, 18, 19, 19, 20, 20)), (DEVIATION, 1, (20, 22)), (INVERT, 1, (21, 23)),
        (NORMALISE, 1, (22, 24, 26, 28, 28, 29, 29, 30)), (OUTER, 1, (24, 26, 28, 29, 29, 30, 30, 31)),
        (UP, 0, (25, 29, 31, 36)), (DOWN, 0, (27, 30, 36, 37)),
        (FOLD, 1, (32, 34, 36, 37)),
        (UP, 1, (39, 40, 41, 46)), (DOWN, 1, (40, 41, 46, 47))):
    for _k, _gap in enumerate(_gaps):
        LATE[_gap] += steps(_kind, _img, _k)

EARLY_LAST = {50: steps(PROJECT, 0, 0, 1, 2, 3),
              51: steps(PROJECT, 0, 4, 5, 6, 7) + steps(DEVIATION, 0, 0, 1),
              52: steps(INVERT, 0, 0) + steps(PROJECT, 1, 0, 1),
              53: steps(INVERT, 0, 1) + steps(NORMALISE, 0, 0, 1) + steps(PROJECT, 1, 2, 3)}
LAST = (steps(PROJECT, 1, 4, 5) + steps(NORMALISE, 0, 2, 3) + steps(OUTER, 0, 0, 1, 2, 3) + steps(DEVIATION, 1, 0)
        + steps(PROJECT, 1, 6, 7) + steps(NORMALISE, 0, 4, 5, 6, 7) + steps(OUTER, 0, 4, 5, 6, 7)
        + steps(DEVIATION, 1, 1) + steps(INVERT, 1, 0) + steps(FOLD, 0, 0) + steps(NORMALISE, 1, 0)
        + steps(FOLD, 0, 1) + steps(NORMALISE, 1, 1) + steps(FOLD, 0, 2) + steps(INVERT, 1, 1) + steps(FOLD, 0, 3)
        + steps(NORMALISE, 1, 2) + steps(UP, 0, 0) + steps(NORMALISE, 1, 3, 4) + steps(UP, 0, 1)
        + steps(NORMALISE, 1, 5) + steps(DOWN, 0, 0) + steps(NORMALISE, 1, 6) + steps(UP, 0, 2)
        + steps(NORMALISE, 1, 7) + steps(DOWN, 0, 1) + steps(OUTER, 1, *range(PROJ)) + steps(FOLD, 1, 0)
        + steps(UP, 0, 3) + steps(FOLD, 1, 1) + steps(DOWN, 0, 2) + steps(FOLD, 1, 2) + steps(DOWN, 0, 3)
        + steps(FOLD, 1, 3) + steps(UP, 1, 0, 1) + steps(DOWN, 1, 0) + steps(UP, 1, 2) + steps(DOWN, 1, 1)
        + steps(UP, 1, 3) + steps(DOWN, 1, 2, 3))


def ring_uses(todo):
    return [s for s in todo if s[0] in (PROJECT, UP, DOWN)]


RING_USES = ring_uses(sum(LATE.values(), []))
RING_LAST = ring_uses(sum(EARLY_LAST.values(), []) + LAST)
assert sorted(RING_USES) == sorted(RING_LAST)
assert len(RING_USES) % RING == 0


def i_is(i, value):
    return isinstance(i, int) and i == value


def conv_attention_kernel(nc, x, w1, b1, w2, b2, qkv_w, o1_w, o2_w, kln_w, kln_b, vln_w, vln_b, out):
    x_v = x.rearrange("(i k) c (j p) w -> i k p c j w", k=2, p=2)
    out_v = out.rearrange("(i k) c (j p) w -> i k p c j w", k=2, p=2)

    ctx = ExitStack()
    with ctx:
        def sb(name, shape, dt=F32):
            return ctx.enter_context(nc.sbuf_tensor(name, shape, dt))

        def sem(name):
            return ctx.enter_context(nc.semaphore(name))

        def pair_of(name, shape, dt=F32):
            return [sb(f"{name}{k}", shape, dt) for k in range(2)]

        x_in_both = sb("x_in", [P, BLOCKS * 2 * 2 * ONE])
        x_in = [x_in_both[:, PIX * k:PIX * (k + 1)].rearrange("p (j w) -> p j w", w=COLS) for k in range(2)]
        x_res = pair_of("x_res", [P, PIX])
        x_hi = pair_of("x_hi", [P, GROUPS, PADDED], F32R)
        x_lo = pair_of("x_lo", [P, GROUPS, PADDED], F32R)
        t_hi = sb("t_hi", [P, SKEWED, PADDED], F32R)
        t_lo = sb("t_lo", [P, SKEWED, PADDED], F32R)
        v_hi = sb("v_hi", [P, QUARTERS, SKEWED, HALF], F32R)
        v_lo = sb("v_lo", [P, QUARTERS, SKEWED, HALF], F32R)
        drain = [sb(f"drain{k}", [P, 8, PADDED]) for k in range(DRAINS)]
        combined = pair_of("combined", [P, QUARTERS * max(SIZES[0]) * HALF])
        f_hi = pair_of("f_hi", [P, PIX], F32R)
        f_lo = pair_of("f_lo", [P, PIX], F32R)
        kv = sb("kv", [P, BLOCKS * 2 * 2, ONE])
        kv_last = x_in_both[:, :].rearrange("p (g c) -> p g c", c=ONE)
        rstd = pair_of("rstd", [P, PROJ, BANK // HD])
        g = pair_of("g", [P, BANK])
        squares = g
        g_hi = pair_of("g_hi", [P, BANK], F32R)
        g_lo = pair_of("g_lo", [P, BANK], F32R)
        y = pair_of("y", [P, BANK])
        w_hi = sb("w_hi", [P, 2 * 2 * K, P], F32R)
        w_lo = sb("w_lo", [P, 2 * 2 * K, P], F32R)
        u_hi = sb("u_hi", [P, 2, 2, P], F32R)
        u_lo = sb("u_lo", [P, 2, 2, P], F32R)
        kvw_hi = sb("kvw_hi", [P, 2 * KV], F32R)
        kvw_lo = sb("kvw_lo", [P, 2 * KV], F32R)
        gw_hi = pair_of("gw_hi", [P, P], F32R)
        gw_lo = pair_of("gw_lo", [P, P], F32R)
        o2_hi = sb("o2_hi", [P, P], F32R)
        o2_lo = sb("o2_lo", [P, P], F32R)
        b1_col = sb("b1_col", [P, 1])
        b2_col = sb("b2_col", [P, 1])
        b2_third = sb("b2_third", [P, 1])
        ident = sb("ident", [P, P])
        ident2 = sb("ident2", [CH, 2, CH])
        head_mask = sb("head_mask", [CH, HEADS, HD])
        k_affine = sb("k_affine", [ONE, CH])
        v_affine = sb("v_affine", [ONE, CH])
        ln_cols = sb("ln_cols", [CH, 2])
        q_w = sb("q_w", [ONE, CH])
        o1_t = sb("o1_t", [CH, CH])
        outer_sb = sb("outer_sb", [ONE, ONE])
        half_affine = outer_sb[:, 0:CH]
        kv_head = sb("kv_head", [ONE, CH])
        mix = ident[0:CH, :].rearrange("p (r c) -> p r c", r=2)
        w_raw = [x_res[k][0:CH, 0:CH * K * K] for k in range(2)]
        w_taps = [x_res[k][0:CH, 1024:1024 + K * (K + 2) * CH].rearrange("o (x s c) -> o x s c", x=K, s=K + 2)
                  for k in range(2)]
        kv_rows = squares[0][:, 0:CH]
        kv_rows2 = squares[0][:, 0:2 * CH].rearrange("o (r c) -> o r c", r=2)
        o_rows = squares[1][0:CH, 0:2 * CH].rearrange("o (r c) -> o r c", r=2)
        o1_rows = squares[1][0:CH, 2 * CH:3 * CH]
        kvw_sum = y[0][:, 0:KV // HD]
        kvw_mean = y[0][:, 64:64 + KV // HD]
        kvw_centred = y[1][:, 0:KV]

        banks = [ctx.enter_context(nc.psum_tensor(f"bank{k}", [P, BANK], F32)) for k in range(8)]
        conv_ps = banks[0:CONV_BANKS]
        ring_ps = banks[CONV_BANKS:CONV_BANKS + RING]
        small_ps = banks[7]
        outer_ps = small_ps[0:ONE, 0:ONE]
        half_ps = small_ps[0:ONE, 128:128 + CH]
        head_ps = small_ps[0:CH, 192:192 + CH]
        mix_ps = small_ps[0:CH, 256:256 + CH]
        gw_ps = small_ps[:, 320:320 + CH]

        w_in = [sem(f"w_in{k}") for k in range(2)]
        biases_in = sem("biases_in")
        rest_in = sem("rest_in")
        zeroed = sem("zeroed")
        ident_made = sem("ident_made")
        consts_made = sem("consts_made")
        taps_ready = sem("taps_ready")
        transposed = sem("transposed")
        w_hi_written = sem("w_hi_written")
        setup_step = sem("setup_step")
        weights_split = sem("weights_split")
        conv_ready = sem("conv_ready")
        drained = sem("drained")
        edge_cleared = sem("edge_cleared")
        value_made = sem("value_made")
        pairs_combined = sem("pairs_combined")
        quarters_combined = sem("quarters_combined")
        hi_written = sem("hi_written")
        conv_out = sem("conv_out")
        x_loaded = [[sem(f"x_loaded{k}_{half}") for half in range(2)] for k in range(2)]
        x_hi_split = sem("x_hi_split")
        x_split = sem("x_split")
        proj_ready = sem("proj_ready")
        proj_taken = sem("proj_taken")
        squares_summed = sem("squares_summed")
        std_ready = sem("std_ready")
        std_eps = sem("std_eps")
        rstd_ready = sem("rstd_ready")
        normalised = sem("normalised")
        small_ready = sem("small_ready")
        gw_hi_written = sem("gw_hi_written")
        small_taken = sem("small_taken")
        up_ready = sem("up_ready")
        gelu_done = sem("gelu_done")
        g_split = sem("g_split")
        down_ready = sem("down_ready")
        down_added = sem("down_added")
        y_ready = sem("y_ready")
        f_hi_added = sem("f_hi_added")
        stored = [sem(f"stored{k}") for k in range(2)]

        def w_ps(xx):
            return ring_ps[xx][:, 0:2 * P].rearrange("p (s o) -> p s o", s=2)

        block = ctx.enter_context(nc.Block())
        REST_DMAS = 3 + 3 + 4
        TAPS_AT, TRANSPOSE_AT, SPLIT_AT = {0: 1, 5: 2}, {1: 1, 6: 2}, {2: 1, 8: 2}

        @block.sync
        def _(sp):
            def load_half(i, k, half):
                groups = slice(16 * half, 16 * half + 16)
                for p in range(2):
                    sp.dma_start(x_in[k][CH * p:CH * p + CH, groups, :], x_v[i, k, p][:, groups, :]
                                 ).then_inc(x_loaded[k][half], 16)

            for half in range(2):
                load_half(0, 0, half)
            for p in range(2):
                sp.dma_start(b1_col[CH * p:CH * p + CH, :], b1.rearrange("(c a) -> c a", a=1)).then_inc(biases_in, 16)
                sp.dma_start(b2_col[CH * p:CH * p + CH, :], b2.rearrange("(c a) -> c a", a=1)).then_inc(biases_in, 16)
            for half in range(2):
                load_half(0, 1, half)
            sp.dma_start(w_raw[1], w2.rearrange("o c y x -> o (c y x)")).then_inc(w_in[1], 16)
            qkv_v = qkv_w.rearrange("(h t d) c -> t h d c", h=HEADS, t=3)
            for t, rows in enumerate((q_w[0:CH, :], kv_rows[0:CH, :], kv_rows[CH:P, :])):
                sp.dma_start(rows, qkv_v[t]).then_inc(rest_in, 16)
            sp.dma_start(o1_rows, o1_w).then_inc(rest_in, 16)
            for r in range(2):
                sp.dma_start(o_rows[:, r, :], o2_w).then_inc(rest_in, 16)
            for k, (w, b, mat) in enumerate(((kln_w, kln_b, k_affine), (vln_w, vln_b, v_affine))):
                sp.dma_start(ln_cols[:, k:k + 1], w.rearrange("h a d -> (h d) a")).then_inc(rest_in, 16)
                sp.dma_start(mat[CH:ONE, :], b.rearrange("h a d -> a (h d)")).then_inc(rest_in, 16)
            for k in range(2):
                sp.sem_inc(stored[k], 32)

            def load(i, k):
                sp.wait_ge(conv_out, i * NC + SLOT_END[2 + k])
                for half in range(2):
                    load_half(i + 1, k, half)

            def store(a, k, c):
                sp.wait_ge(y_ready, a * 2 * TAILS + k * TAILS + c + 1)
                for p in range(2):
                    sp.dma_start(out_v[a, k, p][:, c * 8:c * 8 + 8, :],
                                 y[c % 2][CH * p:CH * p + CH, :].rearrange("c (j w) -> c j w", w=COLS)
                                 ).then_inc(stored[c % 2], 16)

            def iteration(i, loads, stores):
                if loads:
                    load(i, 0)
                    load(i, 1)
                if stores:
                    for k in range(2):
                        for c in range(TAILS):
                            store(i - 1, k, c)

            iteration(0, True, False)
            with sp.Fori(1, PAIRS - 1) as i:
                iteration(i, True, True)
            iteration(PAIRS - 1, False, True)
            iteration(PAIRS, False, True)
            for k in range(2):
                sp.wait_ge(stored[k], 32 * (1 + IMAGES * TAILS // 2))

        @block.gpsimd
        def _(pool):
            nc.gpsimd.memset(ident[:, :], 0.0).then_inc(zeroed, 1)
            pool.wait_ge(zeroed, 1)
            nc.gpsimd.affine_select(out=ident[:, :], in_=ident[:, :], compare_op=ALU.not_equal, fill=1.0,
                                    base=0, pattern=[[-1, P]], channel_multiplier=1).then_inc(ident_made, 1)
            for t in (t_hi, t_lo):
                nc.gpsimd.memset(t[:, :, 0:PADDED:PADDED - 1].bitcast(F32), 0.0).then_inc(consts_made, 1)
            for k in range(DRAINS):
                nc.gpsimd.memset(drain[k][:, :, 0:PADDED:PADDED - 1], 0.0).then_inc(consts_made, 1)
            nc.gpsimd.memset(kv[:, :, CH:ONE], 1.0).then_inc(consts_made, 1)
            nc.gpsimd.memset(head_mask[:, :, :], 1.0 / (ROWS * COLS)).then_inc(zeroed, 1)
            pool.wait_ge(zeroed, 2)
            nc.gpsimd.affine_select(out=head_mask[:, :, :], in_=head_mask[:, :, :], compare_op=ALU.is_ge, fill=0.0,
                                    base=0, pattern=[[-HD, HEADS], [0, HD]], channel_multiplier=1).then_inc(zeroed, 1)
            pool.wait_ge(zeroed, 3)
            nc.gpsimd.affine_select(out=head_mask[:, :, :], in_=head_mask[:, :, :], compare_op=ALU.is_ge, fill=0.0,
                                    base=HD - 1, pattern=[[HD, HEADS], [0, HD]], channel_multiplier=-1
                                    ).then_inc(consts_made, 1)

        @block.scalar
        def _(act):
            act.dma_start(w_raw[0], w1.rearrange("o c y x -> o (c y x)")).then_inc(w_in[0], 16)

            def split_x_hi(i, k, half):
                groups = slice(16 * half, 16 * half + 16)
                act.wait_ge(x_loaded[k][half], 32 * (i + 1))
                nc.scalar.activation(x_hi[k][:, groups, 1:COLS + 1], x_in[k][:, groups, :], ACT.Copy
                                     ).then_inc(x_hi_split, 1)

            def split_w_hi(k):
                act.wait_ge(transposed, k + 1)
                for xx in range(K):
                    at = k * 2 * K + xx
                    nc.scalar.activation(w_hi[:, at:at + K + 1:K, :], w_ps(xx), ACT.Copy).then_inc(w_hi_written, 1)

            split_w_hi(0)
            for half in range(2):
                split_x_hi(0, 0, half)
            act.wait_ge(biases_in, 16 * 4)

            def set_up(n):
                if n == 0:
                    for half in range(2):
                        split_x_hi(0, 1, half)
                if SPLIT_AT.get(n) == 1:
                    split_w_hi(1)

            def drain_conv(i, n):
                slot, img, conv, step, g0, size = CHUNKS[n]
                m = last_use(n)
                for part in range(UNITS[n]):
                    unit = UNIT[n] + part
                    act.wait_ge(conv_ready, i * NU + unit + 1)
                    if part == 0 and not (i_is(i, 0) and m < 0):
                        if made_by_dve(m):
                            act.wait_ge(value_made, i * VALUES + value_number(m))
                        else:
                            act.wait_ge(conv_out, i * NC + m + 1)
                    to = drain[unit % DRAINS][:, 0:size, 1:COLS + 1]
                    bank = conv_ps[unit % CONV_BANKS]
                    at = bank[:, 0:size * COLS].rearrange("p (j w) -> p j w", w=COLS)
                    if conv == 0:
                        if img == 0:
                            nc.scalar.activation(to, at, ACT.Relu, bias=b1_col[:, :])
                            to = t_hi[:, g0:g0 + size, 1:COLS + 1]
                        nc.scalar.activation(to, at, ACT.Relu, bias=b1_col[:, :]).then_inc(drained, 1)
                    elif img == 0:
                        nc.scalar.activation(to, at, ACT.Identity, bias=b2_third[:, :], scale=H_STEP
                                             ).then_inc(drained, 1)
                    else:
                        nc.scalar.activation(to.rearrange("p j (m c) -> p m j c", m=2),
                                             bank[:, :].rearrange("p (m j c) -> p m j c", m=2, c=HALF), ACT.Copy,
                                             scale=H_STEP).then_inc(drained, 1)

            def write_hi(i, n):
                if not made_by_dve(n) or i_is(i, 0) and n < 0:
                    return
                slot, img, conv, step, g0, size = CHUNKS[n % NC]
                groups, pixels = slice(g0, g0 + size), slice(g0 * COLS, (g0 + size) * COLS)
                act.wait_ge(value_made, i * VALUES + value_number(n))
                if conv == 0:
                    nc.scalar.activation(v_hi[:, :, groups, :].rearrange("p q j c -> p q (j c)"),
                                         combined[combined_number(n)][:, 0:QUARTERS * size * HALF].rearrange(
                                             "p (q e) -> p q e", q=QUARTERS), ACT.Copy).then_inc(hi_written, 1)
                elif step < STEPS - 1:
                    nc.scalar.activation(x_hi[img][:, groups, 1:COLS + 1],
                                         x_res[img][:, pixels].rearrange("p (j w) -> p j w", w=COLS), ACT.Copy
                                         ).then_inc(hi_written, 1)
                else:
                    nc.scalar.activation(f_hi[img][:, pixels], x_res[img][:, pixels], ACT.Relu
                                         ).then_inc(hi_written, 1)

            def attention(a, todo, uses):
                for s in todo:
                    kind, img, k = s
                    rows = kv_last if img and uses is RING_LAST else kv
                    if kind == PROJECT:
                        done = a * 2 * PROJ + img * PROJ + k
                        act.wait_ge(proj_ready, done + 1)
                        if img and k == 0 and uses is RING_USES:
                            act.wait_ge(small_ready, a * 10 + 1)
                        ps = ring_ps[uses.index(s) % RING]
                        nc.scalar.activation(rows[:, 2 * PX_BANK * k:2 * PX_BANK * (k + 1), 0:CH],
                                             ps[:, :].rearrange("p (g c) -> p g c", c=CH), ACT.Copy)
                        if img or k >= 2:
                            act.wait_ge(squares_summed, done - 1)
                        nc.scalar.activation(squares[k % 2][:, :], ps[:, :], ACT.Square).then_inc(proj_taken, 1)
                    elif kind == DEVIATION:
                        act.wait_ge(squares_summed, a * 2 * PROJ + img * PROJ + (k + 1) * PROJ // 2)
                        half = slice(k * PROJ // 2, (k + 1) * PROJ // 2)
                        nc.scalar.activation(rstd[img][:, half, :], rstd[img][:, half, :], ACT.Sqrt,
                                             scale=1.0 / (HD - 1)).then_inc(std_ready, 1)
                    elif kind == UP:
                        done = a * 2 * TAILS + img * TAILS + k
                        act.wait_ge(up_ready, done + 1)
                        if img or k >= 2:
                            act.wait_ge(g_split, done - 1)
                            act.wait_ge(down_ready, done - 1)
                        ps = ring_ps[uses.index(s) % RING]
                        nc.scalar.activation(g[k % 2][:, :], ps[:, :], ACT.Gelu)
                        nc.scalar.activation(g_hi[k % 2][:, :], ps[:, :], ACT.Gelu).then_inc(gelu_done, 1)
                    elif kind == DOWN:
                        act.wait_ge(down_added, a * 2 * TAILS + img * TAILS + k + 1)
                        nc.scalar.activation(y[k % 2][:, :], y[k % 2][:, :], ACT.Gelu).then_inc(y_ready, 1)

            def iteration(i, attends, splits, first=False):
                for n in range(NC):
                    drain_conv(i, n)
                    write_hi(i, n - 1)
                    if first:
                        set_up(n)
                    if attends:
                        attention(i - 1, LATE[n], RING_USES)
                    if not splits:
                        attention(i, EARLY_LAST.get(n, []), RING_LAST)
                    if splits and n in X_SPLIT:
                        split_x_hi(i + 1, *X_SPLIT[n])

            iteration(0, attends=False, splits=True, first=True)
            with act.Fori(1, PAIRS - 1) as i:
                iteration(i, attends=True, splits=True)
            iteration(PAIRS - 1, attends=True, splits=False)
            write_hi(PAIRS - 1, NC - 1)
            attention(PAIRS - 1, LAST, RING_LAST)

        @block.vector
        def _(dve):
            v = nc.vector
            steps = 0

            def link(instruction):
                nonlocal steps
                steps += 1
                instruction.then_inc(setup_step, 1)
                dve.wait_ge(setup_step, steps)

            def taps(k):
                v.memset(w_taps[k][:, :, 0, :], 0.0)
                v.memset(w_taps[k][:, :, K + 1, :], 0.0)
                dve.wait_ge(w_in[k], 16)
                raw = w_raw[k].rearrange("o (c y x) -> o y x c", y=K, x=K)
                for r in range(K):
                    last = v.tensor_copy(w_taps[k][:, :, 1 + r, :], raw[:, r if k == 0 else K - 1 - r, :, :])
                return last

            def split_w_lo(k):
                for xx in range(K):
                    at = k * 2 * K + xx
                    dve.wait_ge(w_hi_written, k * K + xx + 1)
                    last = v.tensor_tensor(w_lo[:, at:at + K + 1:K, :], w_ps(xx),
                                           w_hi[:, at:at + K + 1:K, :].bitcast(F32), ALU.subtract)
                return last

            def transform_w():
                outer, full = (combined[k][:, 0:2 * P] for k in range(2))
                flat = [ring_ps[xx][:, 0:2 * P] for xx in range(K)]
                dve.wait_ge(w_hi_written, 2 * K)
                link(v.tensor_copy(outer, flat[0]))
                link(v.tensor_tensor(outer, outer, flat[2], ALU.add))
                for k, op in enumerate((ALU.add, ALU.subtract)):
                    hi, lo = (u[:, k, :, :].rearrange("p s o -> p (s o)") for u in (u_hi, u_lo))
                    link(v.tensor_tensor(full, outer, flat[1], op))
                    link(v.tensor_scalar(hi, full, 0.5, None, ALU.mult))
                    link(v.scalar_tensor_tensor(lo, full, 0.5, hi.bitcast(F32), ALU.mult, ALU.subtract))

            def split_x_lo(i, k, half):
                groups = slice(16 * half, 16 * half + 16)
                dve.wait_ge(x_hi_split, i * 4 + 2 * k + half + 1)
                v.tensor_tensor(x_lo[k][:, groups, 1:COLS + 1], x_in[k][:, groups, :],
                                x_hi[k][:, groups, 1:COLS + 1].bitcast(F32), ALU.subtract).then_inc(x_split, 1)

            def split_small(hi, lo, value):
                link(v.tensor_copy(hi, value))
                return v.tensor_tensor(lo, value, hi.bitcast(F32), ALU.subtract)

            def set_up(n):
                if n == 0:
                    for half in range(2):
                        split_x_lo(0, 1, half)
                if TAPS_AT.get(n) == 1:
                    dve.wait_ge(biases_in, 16 * 4)
                    link(v.tensor_scalar(b2_third[:, :], b2_col[:, :], H_STEP, None, ALU.mult))
                    taps(1).then_inc(taps_ready, 1)
                if SPLIT_AT.get(n) == 1:
                    transform_w()
                    split_w_lo(1).then_inc(weights_split, 1)
                if TAPS_AT.get(n) == 2:
                    for w in (kvw_hi, kvw_lo, *gw_hi, *gw_lo, o2_hi, o2_lo):
                        v.memset(w[:, :].bitcast(F32), 0.0)
                    v.memset(kv_head[CH:ONE, :], 0.0)
                    v.memset(q_w[CH:ONE, :], 0.0)
                    dve.wait_ge(rest_in, 16 * REST_DMAS)
                    v.tensor_copy(kv_rows2[:, 1, :], kv_rows2[:, 0, :])
                    v.tensor_copy(ident2[:, 0, :], ident[0:CH, 0:CH])
                    v.tensor_copy(ident2[:, 1, :], ident[0:CH, 0:CH])
                    v.tensor_scalar(k_affine[0:CH, :], ident[0:CH, 0:CH], ln_cols[:, 0:1], None, ALU.mult)
                    v.tensor_scalar(v_affine[0:CH, :], ident[0:CH, 0:CH], ln_cols[:, 1:2], None, ALU.mult
                                    ).then_inc(taps_ready, 1)
                if SPLIT_AT.get(n) == 2:
                    dve.wait_ge(transposed, 3)
                    heads = banks[7][:, 0:KV].rearrange("p (h d) -> p h d", d=HD)
                    link(v.tensor_reduce(kvw_sum, heads, AX.X, ALU.add))
                    link(v.tensor_scalar(kvw_mean, kvw_sum, 1.0 / HD, None, ALU.mult))
                    link(v.tensor_tensor(kvw_centred.rearrange("p (h d) -> p h d", d=HD), heads,
                                         kvw_mean.rearrange("p (h a) -> p h a", a=1).broadcast_to([P, KV // HD, HD]),
                                         ALU.subtract))
                    for p in range(2):
                        rows = slice(CH * p, CH * p + CH)
                        split_small(kvw_hi[rows, KV * p:KV * p + KV], kvw_lo[rows, KV * p:KV * p + KV],
                                    kvw_centred[rows, :])
                        split_small(o2_hi[rows, CH * p:CH * p + CH], o2_lo[rows, CH * p:CH * p + CH],
                                    banks[7][rows, KV:KV + CH])
                    v.tensor_copy(o1_t[:, :], banks[7][0:CH, KV + CH:KV + 2 * CH]).then_inc(weights_split, 1)

            dve.wait_ge(ident_made, 1)
            taps(0).then_inc(taps_ready, 1)
            for k in range(2):
                for t in (x_hi, x_lo):
                    v.memset(t[k][:, :, 0:PADDED:PADDED - 1].bitcast(F32), 0.0)
            split_w_lo(0).then_inc(weights_split, 1)
            for half in range(2):
                split_x_lo(0, 0, half)
            dve.wait_ge(consts_made, DRAINS + 4)

            def take_conv(i, n):
                slot, img, conv, step, g0, size = CHUNKS[n]
                dve.wait_ge(drained, i * NU + UNIT[n] + UNITS[n])
                block = drain[UNIT[n] % DRAINS]
                value = block[:, 0:size, 1:COLS + 1]
                if conv == 0:
                    before = sum(c[2] == 0 for c in SLOTS[:slot])
                    edges = sum(c[2] == 0 for c in SLOTS)
                    cleared = None
                    if g0 == 0:
                        rows, group = slice(CH, P), 0
                        cleared = 2 * before + 1
                    if g0 + size == SKEWED:
                        rows, group = slice(0, CH), size - 1
                        cleared = 2 * before + 2
                    if cleared:
                        last = v.memset(value[rows, group, :], 0.0)
                        if img == 0:
                            last = v.memset(t_hi[rows, g0 + group, 1:COLS + 1].bitcast(F32), 0.0)
                        last.then_inc(edge_cleared, 1)
                        dve.wait_ge(edge_cleared, i * 2 * edges + cleared)
                    if img == 1:
                        four = combined[combined_number(n)][:, 0:QUARTERS * size * HALF].rearrange(
                            "p (q j c) -> p q j c", q=QUARTERS, c=HALF)
                        left, right = (block[:, 0:size, k:k + COLS].rearrange("p j (c s) -> p s j c", s=2)
                                       for k in (0, 2))
                        even, odd = (block[:, 0:size, 1 + k:COLS + 1:2] for k in range(2))
                        dve.wait_ge(conv_out, i * NC + n - 1)
                        v.tensor_tensor(four[:, 0:4:3], left, right, ALU.subtract)
                        v.tensor_tensor(four[:, 1], even, odd, ALU.add)
                        last = v.tensor_tensor(four[:, 2], odd, even, ALU.subtract)
                        last.then_inc(value_made, 1)
                    return
                groups, pixels = slice(g0, g0 + size), slice(g0 * COLS, (g0 + size) * COLS)
                source = (x_in[img][:, groups, :] if step == 0 else
                          x_res[img][:, pixels].rearrange("p (j w) -> p j w", w=COLS))
                total = x_res[img][:, pixels].rearrange("p (j w) -> p j w", w=COLS)
                if img == 1:
                    m0, m1 = (value[:, :, HALF * k:HALF * (k + 1)] for k in range(2))
                    m2, m3 = (drain[(UNIT[n] + 1) % DRAINS][:, :, 1 + HALF * k:1 + HALF * (k + 1)] for k in range(2))
                    value = combined[combined_number(n)][:, 0:BANK].rearrange("p (q j c) -> p q j c", q=2, c=HALF)
                    source, total = (t.rearrange("p j (c q) -> p q j c", q=2) for t in (source, total))
                    nth = sum(winograd(m) for m in range(n + 1))
                    dve.wait_ge(conv_out, i * NC + n - 1)
                    v.scalar_tensor_tensor(value[:, 0], m1, b2_third[:, :], m2, ALU.add, ALU.add)
                    v.scalar_tensor_tensor(value[:, 1], m1, b2_third[:, :], m2, ALU.add, ALU.subtract
                                           ).then_inc(pairs_combined, 1)
                    dve.wait_ge(pairs_combined, i * STEPS * TAILS + nth)
                    v.tensor_tensor(value[:, 0], value[:, 0], m0, ALU.add)
                    v.tensor_tensor(value[:, 1], value[:, 1], m3, ALU.subtract).then_inc(quarters_combined, 1)
                    dve.wait_ge(quarters_combined, i * STEPS * TAILS + nth)
                v.tensor_tensor(total, value, source, ALU.add).then_inc(value_made, 1)

            def write_lo(i, n):
                if i_is(i, 0) and n < 0:
                    return
                slot, img, conv, step, g0, size = CHUNKS[n % NC]
                groups, pixels = slice(g0, g0 + size), slice(g0 * COLS, (g0 + size) * COLS)
                if made_by_dve(n):
                    dve.wait_ge(hi_written, i * VALUES + value_number(n))
                if conv == 0 and img == 0:
                    value = drain[UNIT[n] % DRAINS][:, 0:size, 1:COLS + 1]
                    hi, lo = (t[:, groups, 1:COLS + 1] for t in (t_hi, t_lo))
                elif conv == 0:
                    value = combined[combined_number(n)][:, 0:QUARTERS * size * HALF].rearrange(
                        "p (q e) -> p q e", q=QUARTERS)
                    hi, lo = (t[:, :, groups, :].rearrange("p q j c -> p q (j c)") for t in (v_hi, v_lo))
                elif step < STEPS - 1:
                    value = x_res[img][:, pixels].rearrange("p (j w) -> p j w", w=COLS)
                    hi, lo = (t[img][:, groups, 1:COLS + 1] for t in (x_hi, x_lo))
                else:
                    v.scalar_tensor_tensor(f_lo[img][:, pixels], x_res[img][:, pixels], 0.0,
                                           f_hi[img][:, pixels].bitcast(F32), ALU.max, ALU.subtract
                                           ).then_inc(conv_out, 1)
                    return
                v.tensor_tensor(lo, value, hi.bitcast(F32), ALU.subtract).then_inc(conv_out, 1)

            def attention(a, todo, uses):
                for s in todo:
                    kind, img, k = s
                    rows = kv_last if img and uses is RING_LAST else kv
                    bank = a * 2 * PROJ + img * PROJ + k
                    tail = a * 2 * TAILS + img * TAILS + k
                    if kind == PROJECT:
                        dve.wait_ge(proj_taken, bank + 1)
                        v.tensor_reduce(rstd[img][:, k, :], squares[k % 2][:, :].rearrange("p (h d) -> p h d", d=HD),
                                        AX.X, ALU.add).then_inc(squares_summed, 1)
                    elif kind == INVERT:
                        half = rstd[img][:, k * PROJ // 2:(k + 1) * PROJ // 2, :]
                        dve.wait_ge(std_ready, a * 4 + img * 2 + k + 1)
                        v.tensor_scalar(half, half, LN_EPS, None, ALU.add).then_inc(std_eps, 1)
                        dve.wait_ge(std_eps, a * 4 + img * 2 + k + 1)
                        v.reciprocal(half, half).then_inc(rstd_ready, 1)
                    elif kind == NORMALISE:
                        dve.wait_ge(rstd_ready, a * 4 + img * 2 + k // (PROJ // 2) + 1)
                        rows = rows[:, 2 * PX_BANK * k:2 * PX_BANK * (k + 1), 0:CH].rearrange("p g (h d) -> p g h d", d=HD)
                        scale = rstd[img][:, k, :].rearrange("p (g h a) -> p g h a", h=HEADS, a=1)
                        v.tensor_tensor(rows, rows, scale.broadcast_to([P, 2 * PX_BANK, HEADS, HD]), ALU.mult
                                        ).then_inc(normalised, 1)
                    elif kind == OUTER and k == PROJ - 1:
                        dve.wait_ge(small_ready, a * 10 + img * 5 + 1)
                        v.tensor_copy(outer_sb[:, :], outer_ps).then_inc(small_taken, 1)
                    elif kind == FOLD:
                        dve.wait_ge(small_ready, a * 10 + img * 5 + k + 2)
                        if k == 0:
                            v.tensor_copy(half_affine, half_ps).then_inc(small_taken, 1)
                        elif k == 1:
                            v.tensor_tensor(kv_head[0:CH, :], head_ps, head_mask[:, :, :].rearrange("p h d -> p (h d)"),
                                            ALU.mult).then_inc(small_taken, 1)
                        elif k == 2:
                            v.tensor_tensor(mix[:, 0, :], mix_ps, ident2[:, 0, :], ALU.add)
                            v.tensor_tensor(mix[:, 1, :], mix_ps, ident2[:, 1, :], ALU.add).then_inc(small_taken, 1)
                        else:
                            for p in range(2):
                                rows = cols = slice(CH * p, CH * p + CH)
                                v.tensor_copy(gw_hi[img][rows, cols], gw_ps[rows, :]).then_inc(gw_hi_written, 1)
                                dve.wait_ge(gw_hi_written, a * 4 + img * 2 + p + 1)
                                low = v.tensor_tensor(gw_lo[img][rows, cols], gw_ps[rows, :],
                                                      gw_hi[img][rows, cols].bitcast(F32), ALU.subtract)
                            low.then_inc(small_taken, 1)
                    elif kind == UP:
                        dve.wait_ge(gelu_done, tail + 1)
                        v.tensor_tensor(g_lo[k % 2][:, :], g[k % 2][:, :], g_hi[k % 2][:, :].bitcast(F32),
                                        ALU.subtract).then_inc(g_split, 1)
                    elif kind == DOWN:
                        dve.wait_ge(down_ready, tail + 1)
                        dve.wait_ge(stored[k % 2], 32 * ((a * 2 + img) * TAILS // 2 + k // 2 + 1))
                        at = slice(BANK * k, BANK * (k + 1))
                        v.tensor_tensor(y[k % 2][:, :], ring_ps[uses.index(s) % RING][:, :],
                                        f_hi[img][:, at].bitcast(F32), ALU.add).then_inc(f_hi_added, 1)
                        dve.wait_ge(f_hi_added, tail + 1)
                        v.tensor_tensor(y[k % 2][:, :], y[k % 2][:, :], f_lo[img][:, at].bitcast(F32), ALU.add
                                        ).then_inc(down_added, 1)

            def iteration(i, attends, splits, first=False):
                for n in range(NC):
                    take_conv(i, n)
                    if made_by_dve(n - 1):
                        write_lo(i, n - 1)
                    if not made_by_dve(n):
                        write_lo(i, n)
                    if not splits and n == SLOT_END[3]:
                        v.memset(kv_last[:, :, CH:ONE], 1.0)
                    if first:
                        set_up(n)
                    if attends:
                        attention(i - 1, LATE[n], RING_USES)
                    if not splits:
                        attention(i, EARLY_LAST.get(n, []), RING_LAST)
                    if splits and n in X_SPLIT:
                        split_x_lo(i + 1, *X_SPLIT[n])

            iteration(0, attends=False, splits=True, first=True)
            with dve.Fori(1, PAIRS - 1) as i:
                iteration(i, attends=True, splits=True)
            iteration(PAIRS - 1, attends=True, splits=False)
            write_lo(PAIRS - 1, NC - 1)
            attention(PAIRS - 1, LAST, RING_LAST)

        @block.tensor
        def _(pe):
            mm = nc.tensor.matmul
            def transpose_taps(k):
                pe.wait_ge(taps_ready, k + 1)
                for xx in range(K):
                    for q in range(4):
                        last = nc.tensor.transpose(w_ps(xx)[:, q // 2, CH * (q % 2):CH * (q % 2 + 1)],
                                                   w_taps[k][:, xx, q:q + 2, :].rearrange("o s c -> o (s c)"),
                                                   ident[0:CH, 0:CH])
                last.then_inc(transposed, 1)

            def transpose_rest():
                pe.wait_ge(taps_ready, 3)
                nc.tensor.transpose(banks[7][:, 0:KV], kv_rows2.rearrange("o r c -> o (r c)"), ident[:, :])
                nc.tensor.transpose(banks[7][:, KV:KV + CH], o_rows.rearrange("o r c -> o (r c)"), ident[0:CH, 0:CH])
                nc.tensor.transpose(banks[7][0:CH, KV + CH:KV + 2 * CH], o1_rows, ident[0:CH, 0:CH]
                                    ).then_inc(transposed, 1)

            def set_up(n):
                if TRANSPOSE_AT.get(n) == 1:
                    transpose_taps(1)
                if TRANSPOSE_AT.get(n) == 2:
                    transpose_rest()

            transpose_taps(0)
            pe.wait_ge(weights_split, 1)

            def three(ps, lhs, rhs, first, last):
                mm(ps, lhs[0], rhs[0], start=first, stop=False)
                mm(ps, lhs[0], rhs[1], start=False, stop=False)
                return mm(ps, lhs[1], rhs[0], start=False, stop=last)

            def products(n, part):
                g0, size = CHUNKS[n][4:]
                for k in range(2):
                    ps = conv_ps[(UNIT[n] + part) % CONV_BANKS][:, k * BANK // 2:(k + 1) * BANK // 2]
                    quarter = 2 * part + k
                    for stack in range(2):
                        at = (2 + 1 - stack) * K + (0 if quarter == 0 else K - 1)
                        lhs = ((w_hi[:, at, :], w_lo[:, at, :]) if quarter in (0, 3) else
                               (u_hi[:, quarter - 1, 1 - stack, :], u_lo[:, quarter - 1, 1 - stack, :]))
                        groups = slice(g0 + stack, g0 + stack + size)
                        last = three(ps, lhs, (v_hi[:, quarter, groups, :], v_lo[:, quarter, groups, :]),
                                     stack == 0, stack == 1)
                return last

            def convolve(i, n):
                slot, img, conv, step, g0, size = CHUNKS[n]
                if slot < 2:
                    pe.wait_ge(x_split, i * 4 + 2 * slot + 1 + (g0 + size >= GROUPS // 2))
                elif g0 == 0:
                    if i_is(i, 0) and slot == 2:
                        pe.wait_ge(weights_split, 2)
                    pe.wait_ge(conv_out, i * NC + SLOT_END[slot - 2])
                for part in range(UNITS[n]):
                    unit = UNIT[n] + part
                    if not (i_is(i, 0) and unit < CONV_BANKS):
                        pe.wait_ge(drained, i * NU + unit - CONV_BANKS + 1)
                    if UNITS[n] == 2:
                        products(n, part).then_inc(conv_ready, 1)
                if UNITS[n] == 2:
                    return
                hi, lo, pad = (x_hi[img], x_lo[img], 1) if conv == 0 else (t_hi, t_lo, 0)
                top, bottom = conv == 0 and g0 == 0, conv == 0 and g0 + size == SKEWED
                for nth, stack in enumerate((1, 0) if top else (0, 1)):
                    skip_first, skip_last = int(top and stack == 0), int(bottom and stack == 1)
                    ps = conv_ps[UNIT[n] % CONV_BANKS][:, skip_first * COLS:(size - skip_last) * COLS]
                    groups = slice(g0 + stack - pad + skip_first, g0 + stack - pad + size - skip_last)
                    for xx in range(K):
                        at = (conv * 2 + (stack if conv == 0 else 1 - stack)) * K + xx
                        cols = slice(xx, xx + COLS)
                        last = three(ps, (w_hi[:, at, :], w_lo[:, at, :]),
                                     (hi[:, groups, cols], lo[:, groups, cols]),
                                     nth == 0 and xx == 0, nth == 1 and xx == K - 1)
                last.then_inc(conv_ready, 1)

            def ring_free(a, s, uses):
                r = uses.index(s)
                if r >= RING or isinstance(a, int) and a > 0:
                    kind, img, k = uses[r - RING] if r >= RING else RING_USES[r - RING]
                    b = a if r >= RING else a - 1
                    if kind == PROJECT:
                        pe.wait_ge(proj_taken, b * 2 * PROJ + img * PROJ + k + 1)
                    elif kind == UP:
                        pe.wait_ge(gelu_done, b * 2 * TAILS + img * TAILS + k + 1)
                    else:
                        pe.wait_ge(down_added, b * 2 * TAILS + img * TAILS + k + 1)
                return ring_ps[r % RING]

            def attention(a, todo, uses):
                for s in todo:
                    kind, img, k = s
                    rows = kv_last if img and uses is RING_LAST else kv
                    tail = a * 2 * TAILS + img * TAILS + k
                    if kind == PROJECT:
                        chunk = SLOT_END[9 + img] + k // 2 if uses is RING_LAST else max(51, SLOT_END[9 + img] + k // 2)
                        pe.wait_ge(conv_out, a * NC + chunk + 1)
                        if i_is(a, 0) and k == 0:
                            pe.wait_ge(weights_split, 3)
                        ps = ring_free(a, s, uses)
                        for j in range(PER_BANK):
                            at = slice(P * (PER_BANK * k + j), P * (PER_BANK * k + j + 1))
                            to = ps[:, 2 * KV * j:2 * KV * (j + 1)]
                            mm(to, f_hi[img][:, at], kvw_hi[:, :], start=True, stop=False)
                            mm(to, f_hi[img][:, at], kvw_lo[:, :], start=False, stop=False)
                            last = mm(to, f_lo[img][:, at], kvw_hi[:, :], start=False, stop=True)
                        last.then_inc(proj_ready, 1)
                    elif kind == OUTER:
                        pe.wait_ge(normalised, a * 2 * PROJ + img * PROJ + k + 1)
                        if img and k == 0:
                            pe.wait_ge(small_taken, a * 10 + 5)
                        for j in range(PX_BANK):
                            at = 2 * (PX_BANK * k + j)
                            last = mm(outer_ps, rows[:, at, :], rows[:, at + 1, :], start=(k == 0 and j == 0),
                                      stop=(k == PROJ - 1 and j == PX_BANK - 1))
                        if k == PROJ - 1:
                            last.then_inc(small_ready, 1)
                    elif kind == FOLD:
                        pe.wait_ge(small_taken, a * 10 + img * 5 + k + 1)
                        if k == 0:
                            last = mm(half_ps, outer_sb[:, :], k_affine[:, :], start=True, stop=True)
                        elif k == 1:
                            last = mm(head_ps, half_affine, v_affine[:, :], start=True, stop=True)
                        elif k == 2:
                            last = mm(mix_ps, kv_head[:, :], q_w[:, :], start=True, stop=True)
                        else:
                            last = mm(gw_ps, ident[0:CH, :], o1_t[:, :],
                                      start=True, stop=True)
                        last.then_inc(small_ready, 1)
                    elif kind == UP:
                        if k == 0:
                            pe.wait_ge(small_taken, a * 10 + img * 5 + 5)
                        at = slice(BANK * k, BANK * (k + 1))
                        three(ring_free(a, s, uses)[:, :], (gw_hi[img][:, :], gw_lo[img][:, :]), (f_hi[img][:, at], f_lo[img][:, at]),
                              True, True).then_inc(up_ready, 1)
                    elif kind == DOWN:
                        pe.wait_ge(g_split, tail + 1)
                        three(ring_free(a, s, uses)[:, :], (o2_hi[:, :], o2_lo[:, :]), (g_hi[k % 2][:, :], g_lo[k % 2][:, :]),
                              True, True).then_inc(down_ready, 1)

            def iteration(i, attends, splits, first=False):
                for n in range(NC):
                    convolve(i, n)
                    if first:
                        set_up(n)
                    if attends:
                        attention(i - 1, LATE[n], RING_USES)
                    if not splits:
                        attention(i, EARLY_LAST.get(n, []), RING_LAST)

            iteration(0, attends=False, splits=True, first=True)
            with pe.Fori(1, PAIRS - 1) as i:
                iteration(i, attends=True, splits=True)
            iteration(PAIRS - 1, attends=True, splits=False)
            attention(PAIRS - 1, LAST, RING_LAST)


_INS = ["x", "L0_conv_w1", "L0_conv_b1", "L0_conv_w2", "L0_conv_b2", "L1_conv_qkv_w", "L1_conv_o1_w", "L1_conv_o2_w",
        "L1_conv_kln_w", "L1_conv_kln_b", "L1_conv_vln_w", "L1_conv_vln_b"]


def kernel(**inputs):
    import numpy as np
    import concourse.bacc as bacc
    from concourse.bass_utils import run_bass_kernel_spmd

    nc = bacc.Bacc("TRN2", target_bir_lowering=False, num_devices=1, dynamic_dma_scratch_size=1024)
    arrays, args = {}, []
    for name in _INS:
        a = np.ascontiguousarray(inputs[name])
        arrays[f"in_{name}"] = a
        args.append(nc.dram_tensor(f"in_{name}", a.shape, mybir.dt.from_np(a.dtype), kind="ExternalInput").ap())
    args.append(nc.dram_tensor("out", (IMAGES, CH, ROWS, COLS), F32, kind="ExternalOutput").ap())
    conv_attention_kernel(nc, *args)
    r = run_bass_kernel_spmd(nc, [arrays], core_ids=[0])
    return r.results[0]["out"]
```

```python
import concourse.bass as bass
from concourse import mybir
from contextlib import ExitStack

F32 = mybir.dt.float32
F32R = mybir.dt.float32r
ALU = mybir.AluOpType
ACT = mybir.ActivationFunctionType
AX = mybir.AxisListType

IMAGES, CH, ROWS, COLS = 16, 64, 64, 64
P = 2 * CH
PAIRS = IMAGES // 2
GROUPS = ROWS // 2
SKEWED = GROUPS + 1
PIX = GROUPS * COLS
STEPS = 3
H_STEP = 1.0 / 3.0
K = 3
PADDED = COLS + 2
BANK = 512

HEADS, HD = 8, 8
KV = 2 * CH
LN_EPS = 1e-5
ONE = CH + 1
BLOCKS = PIX // P
PER_BANK = BANK // (2 * KV)
PROJ = BLOCKS // PER_BANK
PX_BANK = 2 * PER_BANK
TAILS = PIX // BANK

SIZES = ((7, 7, 7, 6, 6), (8, 8, 8, 8))
AHEAD = (1, 2)
SLOTS = [(k, k // 2 % 2, k % 2, k // 4) if k // 4 in AHEAD else (k, k % 2, k // 2 % 2, k // 4)
         for k in range(4 * STEPS)]
CHUNKS = [(slot, img, conv, step, sum(SIZES[conv][:n]), size)
          for slot, img, conv, step in SLOTS for n, size in enumerate(SIZES[conv])]
NC = len(CHUNKS)


def first_chunk(img, conv, step):
    return next(n for n, c in enumerate(CHUNKS) if c[1:4] == (img, conv, step))


FIRST_STEP_END = [first_chunk(img, 1, 0) + len(SIZES[1]) for img in range(2)]
LAST_CONV = [first_chunk(img, 1, STEPS - 1) for img in range(2)]


def needed(n):
    slot, img, conv, step, g0, size = CHUNKS[n]
    group = g0 + size if conv == 1 else min(g0 + size, GROUPS) - 1
    return next(m for m, c in enumerate(CHUNKS) if (c[1], c[2], c[3]) == (img, 1 - conv, step - 1 + conv)
                and c[4] <= group < c[4] + c[5])


CONV_BANKS = 3
RING = 4
QUARTERS = 4
HALF = COLS // 2
TRANSFORMED = ((1,), (0, 1, 2))
assert set(TRANSFORMED[0]) <= set(AHEAD)


def transformed(n):
    return CHUNKS[n % NC][3] in TRANSFORMED[CHUNKS[n % NC][1]]


def winograd(n):
    return CHUNKS[n % NC][2] == 1 and transformed(n)


def made_by_dve(n):
    return CHUNKS[n % NC][2] == 1 or transformed(n)


VALUES = sum(made_by_dve(n) for n in range(NC))


def value_number(n):
    return sum(made_by_dve(m) for m in range(n % NC + 1)) + n // NC * VALUES


def combined_number(n):
    return sum(transformed(m) for m in range(n % NC)) % 2


UNITS = [1 + winograd(n) for n in range(NC)]
UNIT = [sum(UNITS[:n]) for n in range(NC)]
NU = sum(UNITS)


def bank_before(unit):
    return max(u for u in range(unit - NU, unit) if u % NU % CONV_BANKS == unit % CONV_BANKS)


DRAINS = 4


def last_use(n):
    mine = {(UNIT[n] + k) % DRAINS for k in range(UNITS[n])}
    before = [(m, UNIT[m % NC], UNITS[m % NC]) for m in range(n - NC, n)]
    return max(m for m, unit, units in before if mine & {(unit + k) % DRAINS for k in range(units)})


X_SPLIT = ({43: 0, 45: 1}, {0: 0, 2: 1})

PROJECT, DEVIATION, INVERT, NORMALISE, OUTER, FOLD, UP, DOWN, FINISH = (
    "project", "deviation", "invert", "normalise", "outer", "fold", "up", "down", "finish")


def steps(kind, img, *numbers):
    return [(kind, img, k) for k in numbers]


LATE = {n: [] for n in range(NC)}
for _kind, _img, _gaps in (
        (PROJECT, 0, (0, 0, 1, 1, 1, 2, 2, 2)), (DEVIATION, 0, (2, 3)), (INVERT, 0, (3, 4)),
        (NORMALISE, 0, (4, 5, 7, 8, 10, 10, 11, 11)), (OUTER, 0, (6, 7, 9, 10, 11, 12, 12, 13)),
        (FOLD, 0, (14, 16, 18, 20)), (PROJECT, 1, (13, 13, 18, 18, 19, 19, 20, 20)),
        (DEVIATION, 1, (20, 22)), (INVERT, 1, (21, 23)), (NORMALISE, 1, (22, 25, 26, 28, 28, 29, 30, 31)),
        (OUTER, 1, (26, 27, 29, 30, 31, 32, 33, 34)), (UP, 0, (24, 27, 29, 34)), (DOWN, 0, (27, 30, 37, 37)),
        (FOLD, 1, (36, 37, 38, 39)), (UP, 1, (40, 41, 42, 43)), (DOWN, 1, (41, 42, 43, 44))):
    for _k, _gap in enumerate(_gaps):
        LATE[_gap] += steps(_kind, _img, _k) + (steps(FINISH, _img, _k) if _kind == DOWN else [])

EARLY_LAST = {n: [] for n in range(NC)}
for _kind, _gaps in (
        (PROJECT, (44, 44, 45, 45, 46, 46, 47, 47)), (DEVIATION, (46, 48)), (INVERT, (47, 49)),
        (NORMALISE, (48, 49, 50, 51, 52, 53)), (OUTER, (50, 51, 52, 53))):
    for _k, _gap in enumerate(_gaps):
        EARLY_LAST[_gap] += steps(_kind, 0, _k)
EARLY_LAST[52] += steps(PROJECT, 1, 0, 1)
EARLY_LAST[53] += steps(PROJECT, 1, 2, 3)
LAST = (steps(PROJECT, 1, 4, 5) + steps(DEVIATION, 1, 0) + steps(PROJECT, 1, 6, 7)
        + steps(NORMALISE, 0, 6) + steps(INVERT, 1, 0) + steps(DEVIATION, 1, 1) + steps(NORMALISE, 0, 7)
        + steps(OUTER, 0, 4, 5, 6, 7) + steps(INVERT, 1, 1) + steps(FOLD, 0, 0) + steps(NORMALISE, 1, 0)
        + steps(FOLD, 0, 1) + steps(NORMALISE, 1, 1) + steps(FOLD, 0, 2) + steps(NORMALISE, 1, 2)
        + steps(FOLD, 0, 3) + steps(NORMALISE, 1, 3) + steps(UP, 0, 0) + steps(OUTER, 1, 0, 1, 2, 3)
        + steps(NORMALISE, 1, 4) + steps(UP, 0, 1) + steps(NORMALISE, 1, 5) + steps(DOWN, 0, 0)
        + steps(NORMALISE, 1, 6) + steps(UP, 0, 2) + steps(FINISH, 0, 0) + steps(NORMALISE, 1, 7)
        + steps(DOWN, 0, 1) + steps(OUTER, 1, 4, 5, 6, 7) + steps(FOLD, 1, 0) + steps(UP, 0, 3)
        + steps(FINISH, 0, 1) + steps(FOLD, 1, 1) + steps(DOWN, 0, 2) + steps(FINISH, 0, 2)
        + steps(FOLD, 1, 2) + steps(FOLD, 1, 3) + steps(UP, 1, 0) + steps(DOWN, 0, 3)
        + steps(FINISH, 0, 3) + steps(UP, 1, 1) + steps(DOWN, 1, 0) + steps(UP, 1, 2)
        + steps(FINISH, 1, 0) + steps(DOWN, 1, 1) + steps(UP, 1, 3) + steps(FINISH, 1, 1)
        + steps(DOWN, 1, 2) + steps(FINISH, 1, 2) + steps(DOWN, 1, 3) + steps(FINISH, 1, 3))

LATE_END = 1 + max(n for n in range(NC) if LATE[n])


def ring_uses(todo):
    return [s for s in todo if s[0] in (PROJECT, UP, DOWN)]


RING_USES = ring_uses(sum(LATE.values(), []))
RING_LAST = ring_uses(sum(EARLY_LAST.values(), []) + LAST)
assert sorted(RING_USES) == sorted(RING_LAST)
assert len(RING_USES) % RING == 0


def i_is(i, value):
    return isinstance(i, int) and i == value


def conv_attention_kernel(nc, x, w1, b1, w2, b2, qkv_w, o1_w, o2_w, kln_w, kln_b, vln_w, vln_b, out):
    x_v = x.rearrange("(i k) c (j p) w -> i k p c j w", k=2, p=2)
    out_v = out.rearrange("(i k) c (j p) w -> i k p c j w", k=2, p=2)

    ctx = ExitStack()
    with ctx:
        def sb(name, shape, dt=F32):
            return ctx.enter_context(nc.sbuf_tensor(name, shape, dt))

        def sem(name):
            return ctx.enter_context(nc.semaphore(name))

        def pair_of(name, shape, dt=F32):
            return [sb(f"{name}{k}", shape, dt) for k in range(2)]

        x_in_both = sb("x_in", [P, BLOCKS * 2 * 2 * ONE])
        x_in = [x_in_both[:, PIX * k:PIX * (k + 1)].rearrange("p (j w) -> p j w", w=COLS) for k in range(2)]
        x_res = pair_of("x_res", [P, PIX])
        x_hi = pair_of("x_hi", [P, GROUPS, PADDED], F32R)
        x_lo = pair_of("x_lo", [P, GROUPS, PADDED], F32R)
        t_hi = sb("t_hi", [P, SKEWED, PADDED], F32R)
        t_lo = sb("t_lo", [P, SKEWED, PADDED], F32R)
        v_hi = sb("v_hi", [P, QUARTERS, SKEWED, HALF], F32R)
        v_lo = sb("v_lo", [P, QUARTERS, SKEWED, HALF], F32R)
        drain = [sb(f"drain{k}", [P, 8, PADDED]) for k in range(DRAINS)]
        combined = pair_of("combined", [P, QUARTERS * max(SIZES[0]) * HALF])
        f_hi = pair_of("f_hi", [P, PIX], F32R)
        f_lo = pair_of("f_lo", [P, PIX], F32R)
        kv = sb("kv", [P, BLOCKS * 2 * 2, ONE])
        kv_last = x_in_both[:, :].rearrange("p (g c) -> p g c", c=ONE)
        rstd = pair_of("rstd", [P, PROJ, BANK // HD])
        g = pair_of("g", [P, BANK])
        squares = g
        g_hi = pair_of("g_hi", [P, BANK], F32R)
        g_lo = pair_of("g_lo", [P, BANK], F32R)
        y = pair_of("y", [P, BANK])
        w_hi = sb("w_hi", [P, 2 * 2 * K, P], F32R)
        w_lo = sb("w_lo", [P, 2 * 2 * K, P], F32R)
        u_hi = sb("u_hi", [P, 2, 2, P], F32R)
        u_lo = sb("u_lo", [P, 2, 2, P], F32R)
        kvw_hi = sb("kvw_hi", [P, 2 * KV], F32R)
        kvw_lo = sb("kvw_lo", [P, 2 * KV], F32R)
        gw_hi = pair_of("gw_hi", [P, P], F32R)
        gw_lo = pair_of("gw_lo", [P, P], F32R)
        o2_hi = sb("o2_hi", [P, P], F32R)
        o2_lo = sb("o2_lo", [P, P], F32R)
        b1_col = sb("b1_col", [P, 1])
        b2_col = sb("b2_col", [P, 1])
        b2_third = sb("b2_third", [P, 1])
        ident = sb("ident", [P, P])
        ident2 = sb("ident2", [CH, 2, CH])
        head_mask = sb("head_mask", [CH, HEADS, HD])
        k_affine = sb("k_affine", [ONE, CH])
        v_affine = sb("v_affine", [ONE, CH])
        ln_cols = sb("ln_cols", [CH, 2])
        q_w = sb("q_w", [ONE, CH])
        o1_t = sb("o1_t", [CH, CH])
        outer_sb = sb("outer_sb", [ONE, ONE])
        half_affine = outer_sb[:, 0:CH]
        kv_head = sb("kv_head", [ONE, CH])
        mix = ident[0:CH, :].rearrange("p (r c) -> p r c", r=2)
        w_raw = [x_res[k][0:CH, 0:CH * K * K] for k in range(2)]
        w_taps = [x_res[k][0:CH, 1024:1024 + K * (K + 2) * CH].rearrange("o (x s c) -> o x s c", x=K, s=K + 2)
                  for k in range(2)]
        kv_rows = squares[0][:, 0:CH]
        kv_rows2 = squares[0][:, 0:2 * CH].rearrange("o (r c) -> o r c", r=2)
        o_rows = squares[1][0:CH, 0:2 * CH].rearrange("o (r c) -> o r c", r=2)
        o1_rows = squares[1][0:CH, 2 * CH:3 * CH]
        kvw_sum = y[0][:, 0:KV // HD]
        kvw_mean = y[0][:, 64:64 + KV // HD]
        kvw_centred = y[1][:, 0:KV]

        banks = [ctx.enter_context(nc.psum_tensor(f"bank{k}", [P, BANK], F32)) for k in range(8)]
        conv_ps = banks[0:CONV_BANKS]
        ring_ps = banks[CONV_BANKS:CONV_BANKS + RING]
        small_ps = banks[7]
        outer_ps = small_ps[0:ONE, 0:ONE]
        half_ps = small_ps[0:ONE, 128:128 + CH]
        head_ps = small_ps[0:CH, 192:192 + CH]
        mix_ps = small_ps[0:CH, 256:256 + CH]
        gw_ps = small_ps[:, 320:320 + CH]

        w_in = [sem(f"w_in{k}") for k in range(2)]
        biases_in = sem("biases_in")
        rest_in = sem("rest_in")
        zeroed = sem("zeroed")
        ident_made = sem("ident_made")
        consts_made = sem("consts_made")
        taps_ready = sem("taps_ready")
        transposed = sem("transposed")
        w_hi_written = sem("w_hi_written")
        setup_step = sem("setup_step")
        weights_split = sem("weights_split")
        conv_ready = sem("conv_ready")
        drained = sem("drained")
        edge_cleared = sem("edge_cleared")
        value_made = sem("value_made")
        pairs_combined = sem("pairs_combined")
        quarters_combined = sem("quarters_combined")
        hi_written = sem("hi_written")
        conv_out = sem("conv_out")
        x_loaded = [[sem(f"x_loaded{k}_{half}") for half in range(2)] for k in range(2)]
        x_hi_split = sem("x_hi_split")
        x_split = sem("x_split")
        proj_ready = sem("proj_ready")
        proj_taken = sem("proj_taken")
        squares_summed = sem("squares_summed")
        std_ready = sem("std_ready")
        std_eps = sem("std_eps")
        rstd_ready = sem("rstd_ready")
        normalised = sem("normalised")
        small_ready = sem("small_ready")
        gw_hi_written = sem("gw_hi_written")
        small_taken = sem("small_taken")
        up_ready = sem("up_ready")
        gelu_done = sem("gelu_done")
        g_split = sem("g_split")
        down_ready = sem("down_ready")
        down_added = sem("down_added")
        y_ready = sem("y_ready")
        f_hi_added = sem("f_hi_added")
        stored = [sem(f"stored{k}") for k in range(2)]

        def w_ps(xx):
            return ring_ps[xx][:, 0:2 * P].rearrange("p (s o) -> p s o", s=2)

        def result(img, k, last):
            if last and img:
                return drain[k][:, :, 1:COLS + 1]
            return y[k % 2][:, :].rearrange("p (j w) -> p j w", w=COLS)

        block = ctx.enter_context(nc.Block())
        REST_DMAS = 3 + 3 + 4
        TAPS_AT, TRANSPOSE_AT, SPLIT_AT = {0: 1, 5: 2}, {1: 1, 6: 2}, {2: 1, 8: 2}

        @block.sync
        def _(sp):
            def load_half(i, k, half):
                groups = slice(16 * half, 16 * half + 16)
                for p in range(2):
                    sp.dma_start(x_in[k][CH * p:CH * p + CH, groups, :], x_v[i, k, p][:, groups, :]
                                 ).then_inc(x_loaded[k][half], 16)

            for half in range(2):
                load_half(0, 0, half)
            for p in range(2):
                sp.dma_start(b1_col[CH * p:CH * p + CH, :], b1.rearrange("(c a) -> c a", a=1)).then_inc(biases_in, 16)
                sp.dma_start(b2_col[CH * p:CH * p + CH, :], b2.rearrange("(c a) -> c a", a=1)).then_inc(biases_in, 16)
            for half in range(2):
                load_half(0, 1, half)
            sp.dma_start(w_raw[1], w2.rearrange("o c y x -> o (c y x)")).then_inc(w_in[1], 16)
            qkv_v = qkv_w.rearrange("(h t d) c -> t h d c", h=HEADS, t=3)
            for t, rows in enumerate((q_w[0:CH, :], kv_rows[0:CH, :], kv_rows[CH:P, :])):
                sp.dma_start(rows, qkv_v[t]).then_inc(rest_in, 16)
            sp.dma_start(o1_rows, o1_w).then_inc(rest_in, 16)
            for r in range(2):
                sp.dma_start(o_rows[:, r, :], o2_w).then_inc(rest_in, 16)
            for k, (w, b, mat) in enumerate(((kln_w, kln_b, k_affine), (vln_w, vln_b, v_affine))):
                sp.dma_start(ln_cols[:, k:k + 1], w.rearrange("h a d -> (h d) a")).then_inc(rest_in, 16)
                sp.dma_start(mat[CH:ONE, :], b.rearrange("h a d -> a (h d)")).then_inc(rest_in, 16)
            for k in range(2):
                sp.sem_inc(stored[k], 32)

            def load(i, k):
                sp.wait_ge(conv_out, i * NC + FIRST_STEP_END[k])
                for half in range(2):
                    load_half(i + 1, k, half)

            def store(a, k, c, last=False):
                sp.wait_ge(y_ready, a * 2 * TAILS + k * TAILS + c + 1)
                for p in range(2):
                    sp.dma_start(out_v[a, k, p][:, c * 8:c * 8 + 8, :],
                                 result(k, c, last)[CH * p:CH * p + CH, :, :]
                                 ).then_inc(stored[c % 2], 16)

            def iteration(i, loads, stores, last=False):
                if loads:
                    load(i, 0)
                    load(i, 1)
                if stores:
                    for k in range(2):
                        for c in range(TAILS):
                            store(i - 1, k, c, last)

            iteration(0, True, False)
            with sp.Fori(1, PAIRS - 1) as i:
                iteration(i, True, True)
            iteration(PAIRS - 1, False, True)
            iteration(PAIRS, False, True, last=True)
            for k in range(2):
                sp.wait_ge(stored[k], 32 * (1 + IMAGES * TAILS // 2))

        @block.gpsimd
        def _(pool):
            nc.gpsimd.memset(ident[:, :], 0.0).then_inc(zeroed, 1)
            pool.wait_ge(zeroed, 1)
            nc.gpsimd.affine_select(out=ident[:, :], in_=ident[:, :], compare_op=ALU.not_equal, fill=1.0,
                                    base=0, pattern=[[-1, P]], channel_multiplier=1).then_inc(ident_made, 1)
            for t in (t_hi, t_lo):
                nc.gpsimd.memset(t[:, :, 0:PADDED:PADDED - 1].bitcast(F32), 0.0).then_inc(consts_made, 1)
            for k in range(DRAINS):
                nc.gpsimd.memset(drain[k][:, :, 0:PADDED:PADDED - 1], 0.0).then_inc(consts_made, 1)
            nc.gpsimd.memset(kv[:, :, CH:ONE], 1.0).then_inc(consts_made, 1)
            nc.gpsimd.memset(head_mask[:, :, :], 1.0 / (ROWS * COLS)).then_inc(zeroed, 1)
            pool.wait_ge(zeroed, 2)
            nc.gpsimd.affine_select(out=head_mask[:, :, :], in_=head_mask[:, :, :], compare_op=ALU.is_ge, fill=0.0,
                                    base=0, pattern=[[-HD, HEADS], [0, HD]], channel_multiplier=1).then_inc(zeroed, 1)
            pool.wait_ge(zeroed, 3)
            nc.gpsimd.affine_select(out=head_mask[:, :, :], in_=head_mask[:, :, :], compare_op=ALU.is_ge, fill=0.0,
                                    base=HD - 1, pattern=[[HD, HEADS], [0, HD]], channel_multiplier=-1
                                    ).then_inc(consts_made, 1)

        @block.scalar
        def _(act):
            act.dma_start(w_raw[0], w1.rearrange("o c y x -> o (c y x)")).then_inc(w_in[0], 16)

            def split_x_hi(i, k, half):
                groups = slice(16 * half, 16 * half + 16)
                act.wait_ge(x_loaded[k][half], 32 * (i + 1))
                nc.scalar.activation(x_hi[k][:, groups, 1:COLS + 1], x_in[k][:, groups, :], ACT.Copy
                                     ).then_inc(x_hi_split, 1)

            def split_w_hi(k):
                act.wait_ge(transposed, k + 1)
                for xx in range(K):
                    at = k * 2 * K + xx
                    nc.scalar.activation(w_hi[:, at:at + K + 1:K, :], w_ps(xx), ACT.Copy).then_inc(w_hi_written, 1)

            split_w_hi(0)
            for half in range(2):
                split_x_hi(0, 0, half)
            act.wait_ge(biases_in, 16 * 4)

            def set_up(n):
                if n == 0:
                    for half in range(2):
                        split_x_hi(0, 1, half)
                if SPLIT_AT.get(n) == 1:
                    split_w_hi(1)

            def drain_conv(i, n):
                slot, img, conv, step, g0, size = CHUNKS[n]
                m = last_use(n)
                for part in range(UNITS[n]):
                    unit = UNIT[n] + part
                    act.wait_ge(conv_ready, i * NU + unit + 1)
                    if part == 0 and not (i_is(i, 0) and m < 0):
                        if made_by_dve(m):
                            act.wait_ge(value_made, i * VALUES + value_number(m))
                        else:
                            act.wait_ge(conv_out, i * NC + m + 1)
                    to = drain[unit % DRAINS][:, 0:size, 1:COLS + 1]
                    bank = conv_ps[unit % CONV_BANKS]
                    at = bank[:, 0:size * COLS].rearrange("p (j w) -> p j w", w=COLS)
                    if conv == 0:
                        if not transformed(n):
                            nc.scalar.activation(to, at, ACT.Relu, bias=b1_col[:, :])
                            to = t_hi[:, g0:g0 + size, 1:COLS + 1]
                        nc.scalar.activation(to, at, ACT.Relu, bias=b1_col[:, :]).then_inc(drained, 1)
                    elif not transformed(n):
                        nc.scalar.activation(to, at, ACT.Identity, bias=b2_third[:, :], scale=H_STEP
                                             ).then_inc(drained, 1)
                    else:
                        nc.scalar.activation(to.rearrange("p j (m c) -> p m j c", m=2),
                                             bank[:, :].rearrange("p (m j c) -> p m j c", m=2, c=HALF), ACT.Copy,
                                             scale=H_STEP).then_inc(drained, 1)

            def write_hi(i, n):
                if not made_by_dve(n) or i_is(i, 0) and n < 0:
                    return
                slot, img, conv, step, g0, size = CHUNKS[n % NC]
                groups, pixels = slice(g0, g0 + size), slice(g0 * COLS, (g0 + size) * COLS)
                act.wait_ge(value_made, i * VALUES + value_number(n))
                if conv == 0:
                    nc.scalar.activation(v_hi[:, :, groups, :].rearrange("p q j c -> p q (j c)"),
                                         combined[combined_number(n)][:, 0:QUARTERS * size * HALF].rearrange(
                                             "p (q e) -> p q e", q=QUARTERS), ACT.Copy).then_inc(hi_written, 1)
                elif step < STEPS - 1:
                    nc.scalar.activation(x_hi[img][:, groups, 1:COLS + 1],
                                         x_res[img][:, pixels].rearrange("p (j w) -> p j w", w=COLS), ACT.Copy
                                         ).then_inc(hi_written, 1)
                else:
                    nc.scalar.activation(f_hi[img][:, pixels], x_res[img][:, pixels], ACT.Relu
                                         ).then_inc(hi_written, 1)

            def attention(a, todo, uses):
                for s in todo:
                    kind, img, k = s
                    rows = kv_last if img and uses is RING_LAST else kv
                    if kind == PROJECT:
                        done = a * 2 * PROJ + img * PROJ + k
                        act.wait_ge(proj_ready, done + 1)
                        if img and k == 0 and uses is RING_USES:
                            act.wait_ge(small_ready, a * 10 + 1)
                        ps = ring_ps[uses.index(s) % RING]
                        nc.scalar.activation(rows[:, 2 * PX_BANK * k:2 * PX_BANK * (k + 1), 0:CH],
                                             ps[:, :].rearrange("p (g c) -> p g c", c=CH), ACT.Copy)
                        if img or k >= 2:
                            act.wait_ge(squares_summed, done - 1)
                        nc.scalar.activation(squares[k % 2][:, :], ps[:, :], ACT.Square).then_inc(proj_taken, 1)
                    elif kind == DEVIATION:
                        act.wait_ge(squares_summed, a * 2 * PROJ + img * PROJ + (k + 1) * PROJ // 2)
                        half = slice(k * PROJ // 2, (k + 1) * PROJ // 2)
                        nc.scalar.activation(rstd[img][:, half, :], rstd[img][:, half, :], ACT.Sqrt,
                                             scale=1.0 / (HD - 1)).then_inc(std_ready, 1)
                    elif kind == UP:
                        done = a * 2 * TAILS + img * TAILS + k
                        act.wait_ge(up_ready, done + 1)
                        if img or k >= 2:
                            act.wait_ge(g_split, done - 1)
                            act.wait_ge(down_ready, done - 1)
                        ps = ring_ps[uses.index(s) % RING]
                        nc.scalar.activation(g[k % 2][:, :], ps[:, :], ACT.Gelu)
                        nc.scalar.activation(g_hi[k % 2][:, :], ps[:, :], ACT.Gelu).then_inc(gelu_done, 1)
                    elif kind == FINISH:
                        act.wait_ge(down_added, a * 2 * TAILS + img * TAILS + k + 1)
                        to = result(img, k, uses is RING_LAST)
                        nc.scalar.activation(to, to, ACT.Gelu).then_inc(y_ready, 1)

            def iteration(i, attends, splits, first=False):
                for n in range(NC):
                    drain_conv(i, n)
                    write_hi(i, n - 1)
                    if first:
                        set_up(n)
                    if attends:
                        attention(i - 1, LATE[n], RING_USES)
                    if not splits:
                        attention(i, EARLY_LAST.get(n, []), RING_LAST)
                    if splits and n in X_SPLIT[0]:
                        split_x_hi(i + 1, 0, X_SPLIT[0][n])
                    if not first and n in X_SPLIT[1]:
                        split_x_hi(i, 1, X_SPLIT[1][n])

            iteration(0, attends=False, splits=True, first=True)
            with act.Fori(1, PAIRS - 1) as i:
                iteration(i, attends=True, splits=True)
            iteration(PAIRS - 1, attends=True, splits=False)
            write_hi(PAIRS - 1, NC - 1)
            attention(PAIRS - 1, LAST, RING_LAST)

        @block.vector
        def _(dve):
            v = nc.vector
            steps = 0

            def link(instruction):
                nonlocal steps
                steps += 1
                instruction.then_inc(setup_step, 1)
                dve.wait_ge(setup_step, steps)

            def taps(k):
                v.memset(w_taps[k][:, :, 0, :], 0.0)
                v.memset(w_taps[k][:, :, K + 1, :], 0.0)
                dve.wait_ge(w_in[k], 16)
                raw = w_raw[k].rearrange("o (c y x) -> o y x c", y=K, x=K)
                for r in range(K):
                    last = v.tensor_copy(w_taps[k][:, :, 1 + r, :], raw[:, r if k == 0 else K - 1 - r, :, :])
                return last

            def split_w_lo(k):
                for xx in range(K):
                    at = k * 2 * K + xx
                    dve.wait_ge(w_hi_written, k * K + xx + 1)
                    last = v.tensor_tensor(w_lo[:, at:at + K + 1:K, :], w_ps(xx),
                                           w_hi[:, at:at + K + 1:K, :].bitcast(F32), ALU.subtract)
                return last

            def transform_w():
                outer, full = (combined[k][:, 0:2 * P] for k in range(2))
                flat = [ring_ps[xx][:, 0:2 * P] for xx in range(K)]
                dve.wait_ge(w_hi_written, 2 * K)
                link(v.tensor_copy(outer, flat[0]))
                link(v.tensor_tensor(outer, outer, flat[2], ALU.add))
                for k, op in enumerate((ALU.add, ALU.subtract)):
                    hi, lo = (u[:, k, :, :].rearrange("p s o -> p (s o)") for u in (u_hi, u_lo))
                    link(v.tensor_tensor(full, outer, flat[1], op))
                    link(v.tensor_scalar(hi, full, 0.5, None, ALU.mult))
                    link(v.scalar_tensor_tensor(lo, full, 0.5, hi.bitcast(F32), ALU.mult, ALU.subtract))

            def split_x_lo(i, k, half):
                groups = slice(16 * half, 16 * half + 16)
                dve.wait_ge(x_hi_split, i * 4 + 2 * k + half + 1)
                v.tensor_tensor(x_lo[k][:, groups, 1:COLS + 1], x_in[k][:, groups, :],
                                x_hi[k][:, groups, 1:COLS + 1].bitcast(F32), ALU.subtract).then_inc(x_split, 1)

            def split_small(hi, lo, value):
                link(v.tensor_copy(hi, value))
                return v.tensor_tensor(lo, value, hi.bitcast(F32), ALU.subtract)

            def set_up(n):
                if n == 0:
                    for half in range(2):
                        split_x_lo(0, 1, half)
                if TAPS_AT.get(n) == 1:
                    dve.wait_ge(biases_in, 16 * 4)
                    link(v.tensor_scalar(b2_third[:, :], b2_col[:, :], H_STEP, None, ALU.mult))
                    taps(1).then_inc(taps_ready, 1)
                if SPLIT_AT.get(n) == 1:
                    transform_w()
                    split_w_lo(1).then_inc(weights_split, 1)
                if TAPS_AT.get(n) == 2:
                    for w in (kvw_hi, kvw_lo, *gw_hi, *gw_lo, o2_hi, o2_lo):
                        v.memset(w[:, :].bitcast(F32), 0.0)
                    v.memset(kv_head[CH:ONE, :], 0.0)
                    v.memset(q_w[CH:ONE, :], 0.0)
                    dve.wait_ge(rest_in, 16 * REST_DMAS)
                    v.tensor_copy(kv_rows2[:, 1, :], kv_rows2[:, 0, :])
                    v.tensor_copy(ident2[:, 0, :], ident[0:CH, 0:CH])
                    v.tensor_copy(ident2[:, 1, :], ident[0:CH, 0:CH])
                    v.tensor_scalar(k_affine[0:CH, :], ident[0:CH, 0:CH], ln_cols[:, 0:1], None, ALU.mult)
                    v.tensor_scalar(v_affine[0:CH, :], ident[0:CH, 0:CH], ln_cols[:, 1:2], None, ALU.mult
                                    ).then_inc(taps_ready, 1)
                if SPLIT_AT.get(n) == 2:
                    dve.wait_ge(transposed, 3)
                    heads = banks[7][:, 0:KV].rearrange("p (h d) -> p h d", d=HD)
                    link(v.tensor_reduce(kvw_sum, heads, AX.X, ALU.add))
                    link(v.tensor_scalar(kvw_mean, kvw_sum, 1.0 / HD, None, ALU.mult))
                    link(v.tensor_tensor(kvw_centred.rearrange("p (h d) -> p h d", d=HD), heads,
                                         kvw_mean.rearrange("p (h a) -> p h a", a=1).broadcast_to([P, KV // HD, HD]),
                                         ALU.subtract))
                    for p in range(2):
                        rows = slice(CH * p, CH * p + CH)
                        split_small(kvw_hi[rows, KV * p:KV * p + KV], kvw_lo[rows, KV * p:KV * p + KV],
                                    kvw_centred[rows, :])
                        split_small(o2_hi[rows, CH * p:CH * p + CH], o2_lo[rows, CH * p:CH * p + CH],
                                    banks[7][rows, KV:KV + CH])
                    v.tensor_copy(o1_t[:, :], banks[7][0:CH, KV + CH:KV + 2 * CH]).then_inc(weights_split, 1)

            dve.wait_ge(ident_made, 1)
            taps(0).then_inc(taps_ready, 1)
            for k in range(2):
                for t in (x_hi, x_lo):
                    v.memset(t[k][:, :, 0:PADDED:PADDED - 1].bitcast(F32), 0.0)
            split_w_lo(0).then_inc(weights_split, 1)
            for half in range(2):
                split_x_lo(0, 0, half)
            dve.wait_ge(consts_made, DRAINS + 4)

            def take_conv(i, n):
                slot, img, conv, step, g0, size = CHUNKS[n]
                dve.wait_ge(drained, i * NU + UNIT[n] + UNITS[n])
                block = drain[UNIT[n] % DRAINS]
                value = block[:, 0:size, 1:COLS + 1]
                if conv == 0:
                    before = sum(c[2] == 0 for c in SLOTS[:slot])
                    edges = sum(c[2] == 0 for c in SLOTS)
                    cleared = None
                    if g0 == 0:
                        rows, group = slice(CH, P), 0
                        cleared = 2 * before + 1
                    if g0 + size == SKEWED:
                        rows, group = slice(0, CH), size - 1
                        cleared = 2 * before + 2
                    if cleared:
                        last = v.memset(value[rows, group, :], 0.0)
                        if not transformed(n):
                            last = v.memset(t_hi[rows, g0 + group, 1:COLS + 1].bitcast(F32), 0.0)
                        last.then_inc(edge_cleared, 1)
                        dve.wait_ge(edge_cleared, i * 2 * edges + cleared)
                    if transformed(n):
                        four = combined[combined_number(n)][:, 0:QUARTERS * size * HALF].rearrange(
                            "p (q j c) -> p q j c", q=QUARTERS, c=HALF)
                        left, right = (block[:, 0:size, k:k + COLS].rearrange("p j (c s) -> p s j c", s=2)
                                       for k in (0, 2))
                        even, odd = (block[:, 0:size, 1 + k:COLS + 1:2] for k in range(2))
                        dve.wait_ge(conv_out, i * NC + n - 1)
                        v.tensor_tensor(four[:, 0:4:3], left, right, ALU.subtract)
                        v.tensor_tensor(four[:, 1], even, odd, ALU.add)
                        last = v.tensor_tensor(four[:, 2], odd, even, ALU.subtract)
                        last.then_inc(value_made, 1)
                    return
                groups, pixels = slice(g0, g0 + size), slice(g0 * COLS, (g0 + size) * COLS)
                source = (x_in[img][:, groups, :] if step == 0 else
                          x_res[img][:, pixels].rearrange("p (j w) -> p j w", w=COLS))
                total = x_res[img][:, pixels].rearrange("p (j w) -> p j w", w=COLS)
                if transformed(n):
                    m0, m1 = (value[:, :, HALF * k:HALF * (k + 1)] for k in range(2))
                    m2, m3 = (drain[(UNIT[n] + 1) % DRAINS][:, :, 1 + HALF * k:1 + HALF * (k + 1)] for k in range(2))
                    value = combined[combined_number(n)][:, 0:BANK].rearrange("p (q j c) -> p q j c", q=2, c=HALF)
                    source, total = (t.rearrange("p j (c q) -> p q j c", q=2) for t in (source, total))
                    nth = sum(winograd(m) for m in range(n + 1))
                    dve.wait_ge(conv_out, i * NC + n - 1)
                    v.scalar_tensor_tensor(value[:, 0], m1, b2_third[:, :], m2, ALU.add, ALU.add)
                    v.scalar_tensor_tensor(value[:, 1], m1, b2_third[:, :], m2, ALU.add, ALU.subtract
                                           ).then_inc(pairs_combined, 1)
                    dve.wait_ge(pairs_combined, i * sum(winograd(m) for m in range(NC)) + nth)
                    v.tensor_tensor(value[:, 0], value[:, 0], m0, ALU.add)
                    v.tensor_tensor(value[:, 1], value[:, 1], m3, ALU.subtract).then_inc(quarters_combined, 1)
                    dve.wait_ge(quarters_combined, i * sum(winograd(m) for m in range(NC)) + nth)
                v.tensor_tensor(total, value, source, ALU.add).then_inc(value_made, 1)

            def write_lo(i, n):
                if i_is(i, 0) and n < 0:
                    return
                slot, img, conv, step, g0, size = CHUNKS[n % NC]
                groups, pixels = slice(g0, g0 + size), slice(g0 * COLS, (g0 + size) * COLS)
                if made_by_dve(n):
                    dve.wait_ge(hi_written, i * VALUES + value_number(n))
                if conv == 0 and not transformed(n):
                    value = drain[UNIT[n] % DRAINS][:, 0:size, 1:COLS + 1]
                    hi, lo = (t[:, groups, 1:COLS + 1] for t in (t_hi, t_lo))
                elif conv == 0:
                    value = combined[combined_number(n)][:, 0:QUARTERS * size * HALF].rearrange(
                        "p (q e) -> p q e", q=QUARTERS)
                    hi, lo = (t[:, :, groups, :].rearrange("p q j c -> p q (j c)") for t in (v_hi, v_lo))
                elif step < STEPS - 1:
                    value = x_res[img][:, pixels].rearrange("p (j w) -> p j w", w=COLS)
                    hi, lo = (t[img][:, groups, 1:COLS + 1] for t in (x_hi, x_lo))
                else:
                    v.scalar_tensor_tensor(f_lo[img][:, pixels], x_res[img][:, pixels], 0.0,
                                           f_hi[img][:, pixels].bitcast(F32), ALU.max, ALU.subtract
                                           ).then_inc(conv_out, 1)
                    return
                v.tensor_tensor(lo, value, hi.bitcast(F32), ALU.subtract).then_inc(conv_out, 1)

            def attention(a, todo, uses):
                for s in todo:
                    kind, img, k = s
                    rows = kv_last if img and uses is RING_LAST else kv
                    bank = a * 2 * PROJ + img * PROJ + k
                    tail = a * 2 * TAILS + img * TAILS + k
                    if kind == PROJECT:
                        dve.wait_ge(proj_taken, bank + 1)
                        v.tensor_reduce(rstd[img][:, k, :], squares[k % 2][:, :].rearrange("p (h d) -> p h d", d=HD),
                                        AX.X, ALU.add).then_inc(squares_summed, 1)
                    elif kind == INVERT:
                        half = rstd[img][:, k * PROJ // 2:(k + 1) * PROJ // 2, :]
                        dve.wait_ge(std_ready, a * 4 + img * 2 + k + 1)
                        v.tensor_scalar(half, half, LN_EPS, None, ALU.add).then_inc(std_eps, 1)
                        dve.wait_ge(std_eps, a * 4 + img * 2 + k + 1)
                        v.reciprocal(half, half).then_inc(rstd_ready, 1)
                    elif kind == NORMALISE:
                        dve.wait_ge(rstd_ready, a * 4 + img * 2 + k // (PROJ // 2) + 1)
                        rows = rows[:, 2 * PX_BANK * k:2 * PX_BANK * (k + 1), 0:CH].rearrange(
                            "p g (h d) -> p g h d", d=HD)
                        scale = rstd[img][:, k, :].rearrange("p (g h a) -> p g h a", h=HEADS, a=1)
                        v.tensor_tensor(rows, rows, scale.broadcast_to([P, 2 * PX_BANK, HEADS, HD]), ALU.mult
                                        ).then_inc(normalised, 1)
                    elif kind == OUTER and k == PROJ - 1:
                        dve.wait_ge(small_ready, a * 10 + img * 5 + 1)
                        v.tensor_copy(outer_sb[:, :], outer_ps).then_inc(small_taken, 1)
                    elif kind == FOLD:
                        dve.wait_ge(small_ready, a * 10 + img * 5 + k + 2)
                        if k == 0:
                            v.tensor_copy(half_affine, half_ps).then_inc(small_taken, 1)
                        elif k == 1:
                            v.tensor_tensor(kv_head[0:CH, :], head_ps, head_mask[:, :, :].rearrange("p h d -> p (h d)"),
                                            ALU.mult).then_inc(small_taken, 1)
                        elif k == 2:
                            v.tensor_tensor(mix[:, 0, :], mix_ps, ident2[:, 0, :], ALU.add)
                            v.tensor_tensor(mix[:, 1, :], mix_ps, ident2[:, 1, :], ALU.add).then_inc(small_taken, 1)
                        else:
                            for p in range(2):
                                rows = cols = slice(CH * p, CH * p + CH)
                                v.tensor_copy(gw_hi[img][rows, cols], gw_ps[rows, :]).then_inc(gw_hi_written, 1)
                                dve.wait_ge(gw_hi_written, a * 4 + img * 2 + p + 1)
                                low = v.tensor_tensor(gw_lo[img][rows, cols], gw_ps[rows, :],
                                                      gw_hi[img][rows, cols].bitcast(F32), ALU.subtract)
                            low.then_inc(small_taken, 1)
                    elif kind == UP:
                        dve.wait_ge(gelu_done, tail + 1)
                        v.tensor_tensor(g_lo[k % 2][:, :], g[k % 2][:, :], g_hi[k % 2][:, :].bitcast(F32),
                                        ALU.subtract).then_inc(g_split, 1)
                    elif kind == DOWN:
                        dve.wait_ge(down_ready, tail + 1)
                        if not (img and uses is RING_LAST):
                            dve.wait_ge(stored[k % 2], 32 * ((a * 2 + img) * TAILS // 2 + k // 2 + 1))
                        at = slice(BANK * k, BANK * (k + 1))
                        ps = ring_ps[uses.index(s) % RING]
                        if uses is RING_LAST:
                            at, ps = (t.rearrange("p (j w) -> p j w", w=COLS) for t in (x_res[img][:, at], ps[:, :]))
                            v.scalar_tensor_tensor(result(img, k, True), at, 0.0, ps, ALU.max, ALU.add
                                                   ).then_inc(down_added, 1)
                            continue
                        v.tensor_tensor(y[k % 2][:, :], ps[:, :], f_hi[img][:, at].bitcast(F32), ALU.add
                                        ).then_inc(f_hi_added, 1)
                        dve.wait_ge(f_hi_added, tail + 1)
                        v.tensor_tensor(y[k % 2][:, :], y[k % 2][:, :], f_lo[img][:, at].bitcast(F32), ALU.add
                                        ).then_inc(down_added, 1)

            def iteration(i, attends, splits, first=False):
                for n in range(NC):
                    take_conv(i, n)
                    if made_by_dve(n - 1):
                        write_lo(i, n - 1)
                    if not made_by_dve(n):
                        write_lo(i, n)
                    if not splits and n == FIRST_STEP_END[1]:
                        v.memset(kv_last[:, :, CH:ONE], 1.0)
                    if first:
                        set_up(n)
                    if attends:
                        attention(i - 1, LATE[n], RING_USES)
                    if not splits:
                        attention(i, EARLY_LAST.get(n, []), RING_LAST)
                    if splits and n in X_SPLIT[0]:
                        split_x_lo(i + 1, 0, X_SPLIT[0][n])
                    if not first and n in X_SPLIT[1]:
                        split_x_lo(i, 1, X_SPLIT[1][n])

            iteration(0, attends=False, splits=True, first=True)
            with dve.Fori(1, PAIRS - 1) as i:
                iteration(i, attends=True, splits=True)
            iteration(PAIRS - 1, attends=True, splits=False)
            write_lo(PAIRS - 1, NC - 1)
            attention(PAIRS - 1, LAST, RING_LAST)

        @block.tensor
        def _(pe):
            mm = nc.tensor.matmul
            def transpose_taps(k):
                pe.wait_ge(taps_ready, k + 1)
                for xx in range(K):
                    for q in range(4):
                        last = nc.tensor.transpose(w_ps(xx)[:, q // 2, CH * (q % 2):CH * (q % 2 + 1)],
                                                   w_taps[k][:, xx, q:q + 2, :].rearrange("o s c -> o (s c)"),
                                                   ident[0:CH, 0:CH])
                last.then_inc(transposed, 1)

            def transpose_rest():
                pe.wait_ge(taps_ready, 3)
                nc.tensor.transpose(banks[7][:, 0:KV], kv_rows2.rearrange("o r c -> o (r c)"), ident[:, :])
                nc.tensor.transpose(banks[7][:, KV:KV + CH], o_rows.rearrange("o r c -> o (r c)"), ident[0:CH, 0:CH])
                nc.tensor.transpose(banks[7][0:CH, KV + CH:KV + 2 * CH], o1_rows, ident[0:CH, 0:CH]
                                    ).then_inc(transposed, 1)

            def set_up(n):
                if TRANSPOSE_AT.get(n) == 1:
                    transpose_taps(1)
                if TRANSPOSE_AT.get(n) == 2:
                    transpose_rest()

            transpose_taps(0)
            pe.wait_ge(weights_split, 1)

            def three(ps, lhs, rhs, first, last):
                mm(ps, lhs[0], rhs[0], start=first, stop=False)
                mm(ps, lhs[0], rhs[1], start=False, stop=False)
                return mm(ps, lhs[1], rhs[0], start=False, stop=last)

            def products(n, part):
                g0, size = CHUNKS[n][4:]
                for k in range(2):
                    ps = conv_ps[(UNIT[n] + part) % CONV_BANKS][:, k * BANK // 2:(k + 1) * BANK // 2]
                    quarter = 2 * part + k
                    for stack in range(2):
                        at = (2 + 1 - stack) * K + (0 if quarter == 0 else K - 1)
                        lhs = ((w_hi[:, at, :], w_lo[:, at, :]) if quarter in (0, 3) else
                               (u_hi[:, quarter - 1, 1 - stack, :], u_lo[:, quarter - 1, 1 - stack, :]))
                        groups = slice(g0 + stack, g0 + stack + size)
                        last = three(ps, lhs, (v_hi[:, quarter, groups, :], v_lo[:, quarter, groups, :]),
                                     stack == 0, stack == 1)
                return last

            def convolve(i, n):
                slot, img, conv, step, g0, size = CHUNKS[n]
                if conv == 0 and step == 0:
                    pe.wait_ge(x_split, i * 4 + 2 * img + 1 + (g0 + size >= GROUPS // 2))
                else:
                    if i_is(i, 0) and n == first_chunk(0, 1, 0):
                        pe.wait_ge(weights_split, 2)
                    pe.wait_ge(conv_out, i * NC + needed(n) + 1)
                for part in range(UNITS[n]):
                    unit = UNIT[n] + part
                    if not (i_is(i, 0) and bank_before(unit) < 0):
                        pe.wait_ge(drained, i * NU + bank_before(unit) + 1)
                    if UNITS[n] == 2:
                        products(n, part).then_inc(conv_ready, 1)
                if UNITS[n] == 2:
                    return
                hi, lo, pad = (x_hi[img], x_lo[img], 1) if conv == 0 else (t_hi, t_lo, 0)
                top, bottom = conv == 0 and g0 == 0, conv == 0 and g0 + size == SKEWED
                for nth, stack in enumerate((1, 0) if top else (0, 1)):
                    skip_first, skip_last = int(top and stack == 0), int(bottom and stack == 1)
                    ps = conv_ps[UNIT[n] % CONV_BANKS][:, skip_first * COLS:(size - skip_last) * COLS]
                    groups = slice(g0 + stack - pad + skip_first, g0 + stack - pad + size - skip_last)
                    for xx in range(K):
                        at = (conv * 2 + (stack if conv == 0 else 1 - stack)) * K + xx
                        cols = slice(xx, xx + COLS)
                        last = three(ps, (w_hi[:, at, :], w_lo[:, at, :]),
                                     (hi[:, groups, cols], lo[:, groups, cols]),
                                     nth == 0 and xx == 0, nth == 1 and xx == K - 1)
                last.then_inc(conv_ready, 1)

            def ring_free(a, s, uses):
                r = uses.index(s)
                if r >= RING or isinstance(a, int) and a > 0:
                    kind, img, k = uses[r - RING] if r >= RING else RING_USES[r - RING]
                    b = a if r >= RING else a - 1
                    if kind == PROJECT:
                        pe.wait_ge(proj_taken, b * 2 * PROJ + img * PROJ + k + 1)
                    elif kind == UP:
                        pe.wait_ge(gelu_done, b * 2 * TAILS + img * TAILS + k + 1)
                    else:
                        pe.wait_ge(down_added, b * 2 * TAILS + img * TAILS + k + 1)
                return ring_ps[r % RING]

            def attention(a, todo, uses):
                for s in todo:
                    kind, img, k = s
                    rows = kv_last if img and uses is RING_LAST else kv
                    tail = a * 2 * TAILS + img * TAILS + k
                    if kind == PROJECT:
                        chunk = LAST_CONV[img] + k // 2
                        pe.wait_ge(conv_out, a * NC + (chunk if uses is RING_LAST else max(LATE_END, chunk)) + 1)
                        ps = ring_free(a, s, uses)
                        for j in range(PER_BANK):
                            at = slice(P * (PER_BANK * k + j), P * (PER_BANK * k + j + 1))
                            to = ps[:, 2 * KV * j:2 * KV * (j + 1)]
                            mm(to, f_hi[img][:, at], kvw_hi[:, :], start=True, stop=False)
                            mm(to, f_hi[img][:, at], kvw_lo[:, :], start=False, stop=False)
                            last = mm(to, f_lo[img][:, at], kvw_hi[:, :], start=False, stop=True)
                        last.then_inc(proj_ready, 1)
                    elif kind == OUTER:
                        pe.wait_ge(normalised, a * 2 * PROJ + img * PROJ + k + 1)
                        if img and k == 0:
                            pe.wait_ge(small_taken, a * 10 + 5)
                        for j in range(PX_BANK):
                            at = 2 * (PX_BANK * k + j)
                            last = mm(outer_ps, rows[:, at, :], rows[:, at + 1, :], start=(k == 0 and j == 0),
                                      stop=(k == PROJ - 1 and j == PX_BANK - 1))
                        if k == PROJ - 1:
                            last.then_inc(small_ready, 1)
                    elif kind == FOLD:
                        pe.wait_ge(small_taken, a * 10 + img * 5 + k + 1)
                        if k == 0:
                            last = mm(half_ps, outer_sb[:, :], k_affine[:, :], start=True, stop=True)
                        elif k == 1:
                            last = mm(head_ps, half_affine, v_affine[:, :], start=True, stop=True)
                        elif k == 2:
                            last = mm(mix_ps, kv_head[:, :], q_w[:, :], start=True, stop=True)
                        else:
                            last = mm(gw_ps, ident[0:CH, :], o1_t[:, :],
                                      start=True, stop=True)
                        last.then_inc(small_ready, 1)
                    elif kind == UP:
                        if k == 0:
                            pe.wait_ge(small_taken, a * 10 + img * 5 + 5)
                        at = slice(BANK * k, BANK * (k + 1))
                        three(ring_free(a, s, uses)[:, :], (gw_hi[img][:, :], gw_lo[img][:, :]),
                              (f_hi[img][:, at], f_lo[img][:, at]),
                              True, True).then_inc(up_ready, 1)
                    elif kind == DOWN:
                        pe.wait_ge(g_split, tail + 1)
                        three(ring_free(a, s, uses)[:, :], (o2_hi[:, :], o2_lo[:, :]),
                              (g_hi[k % 2][:, :], g_lo[k % 2][:, :]),
                              True, True).then_inc(down_ready, 1)

            def iteration(i, attends, splits, first=False):
                for n in range(NC):
                    convolve(i, n)
                    if first:
                        set_up(n)
                    if attends:
                        attention(i - 1, LATE[n], RING_USES)
                    if not splits:
                        attention(i, EARLY_LAST.get(n, []), RING_LAST)

            iteration(0, attends=False, splits=True, first=True)
            with pe.Fori(1, PAIRS - 1) as i:
                iteration(i, attends=True, splits=True)
            iteration(PAIRS - 1, attends=True, splits=False)
            attention(PAIRS - 1, LAST, RING_LAST)


_INS = ["x", "L0_conv_w1", "L0_conv_b1", "L0_conv_w2", "L0_conv_b2", "L1_conv_qkv_w", "L1_conv_o1_w", "L1_conv_o2_w",
        "L1_conv_kln_w", "L1_conv_kln_b", "L1_conv_vln_w", "L1_conv_vln_b"]


def kernel(**inputs):
    import numpy as np
    import concourse.bacc as bacc
    from concourse.bass_utils import run_bass_kernel_spmd

    nc = bacc.Bacc("TRN2", target_bir_lowering=False, num_devices=1, dynamic_dma_scratch_size=1024)
    arrays, args = {}, []
    for name in _INS:
        a = np.ascontiguousarray(inputs[name])
        arrays[f"in_{name}"] = a
        args.append(nc.dram_tensor(f"in_{name}", a.shape, mybir.dt.from_np(a.dtype), kind="ExternalInput").ap())
    args.append(nc.dram_tensor("out", (IMAGES, CH, ROWS, COLS), F32, kind="ExternalOutput").ap())
    conv_attention_kernel(nc, *args)
    r = run_bass_kernel_spmd(nc, [arrays], core_ids=[0])
    return r.results[0]["out"]
```
